# Optimizing a Trainium2 kernel written in Bass

```python
import numpy as np
import jax
import jax.numpy as jnp

def _softmax(x, axis=-1):
    return jax.nn.softmax(x, axis=axis)

def _gelu(x):
    return jax.nn.gelu(x, approximate=True)

def _silu(x):
    return jax.nn.silu(x)

def _sigmoid(x):
    return jax.nn.sigmoid(x)

def _layernorm(x, axis=-1, eps=1e-05):
    m = jnp.mean(x, axis=axis, keepdims=True)
    v = jnp.var(x, axis=axis, keepdims=True)
    return (x - m) / jnp.sqrt(v + eps)

def _scatter_add(tgt, idx, src, axis=0):
    return tgt.at[idx].add(src)

def _segment_sum(src, seg, n):
    return jax.ops.segment_sum(src, seg, n)
kernel_name = 'mk_cond_resid_d2_seqx_r4_8445fe'

def setup_inputs(seed: int=0):
    np.random.seed(seed)
    _w = jnp.asarray

    def _rec_inputs():
        import jax
        import jax.numpy as jnp
        _rk = jax.random.key(seed)
        x = -0.000125 + 0.9999 * jax.random.normal(jax.random.fold_in(_rk, 1), (8, 256, 1024), jnp.float32)
        _lenS = 256 - jax.random.randint(jax.random.fold_in(_rk, 7), (8,), 0, max(1, 256 // 4) + 1, jnp.int32)
        _lenS2 = 256 - jax.random.randint(jax.random.fold_in(_rk, 8), (8,), 0, max(1, 256 // 4) + 1, jnp.int32)
        itok_B_0_23 = jax.random.randint(jax.random.fold_in(_rk, 11), (8,), 0, 24, jnp.int32)
        itok_B_0_7 = jax.random.randint(jax.random.fold_in(_rk, 12), (8,), 0, 8, jnp.int32)
        return (x, itok_B_0_23, itok_B_0_7)
    x, itok_B_0_23, itok_B_0_7 = _rec_inputs()

    def _L0_cond_setup():
        import jax, jax.numpy as jnp
        import numpy as np
        R = 16
        ALPHA = 32
        SCALING = ALPHA / R
        SLOTS = 32
        IN_F = 1024
        OUT_F = 1024
        B, T = (8, 256)
        key = jax.random.key(seed)
        k1, k2, k3, k4, k5, k6 = jax.random.split(key, 6)
        x = jax.random.normal(k1, (B, T, IN_F), dtype=jnp.float32)
        adapter_mapping = jax.random.randint(k2, (B,), 0, SLOTS, dtype=jnp.int32)
        W = jax.random.normal(k3, (OUT_F, IN_F), dtype=jnp.float32) * 0.02
        b = jax.random.normal(k4, (OUT_F,), dtype=jnp.float32) * 0.02
        lora_As = jax.random.normal(k5, (SLOTS, IN_F, R), dtype=jnp.float32) * 0.02
        lora_Bs = jax.random.normal(k6, (SLOTS, R, OUT_F), dtype=jnp.float32) * 0.02
        return {'x': x, 'adapter_mapping': adapter_mapping, 'W': W, 'b': b, 'lora_As': lora_As, 'lora_Bs': lora_Bs}
    _L0_cond_all = _L0_cond_setup()
    _L0_cond_in = {k: v for k, v in _L0_cond_all.items() if k in ('W', 'b', 'lora_As', 'lora_Bs')}
    del _L0_cond_all

    def _L1_cond_setup():
        import jax, jax.numpy as jnp
        import numpy as np
        TOP_K = 2
        LANG_BIAS = 5.0
        SCALING = 32.0 / 16.0
        LANGUAGE_PAD_ID = -1
        key = jax.random.key(seed)
        ks = jax.random.split(key, 6)
        B, T, D, O, E, R = (4, 512, 1024, 1024, 8, 16)
        x = jax.random.normal(ks[0], (B, T, D), dtype=jnp.float32)
        language_ids = jax.random.randint(ks[1], (B,), 0, E).astype(jnp.int64)
        W = jax.random.normal(ks[2], (O, D), dtype=jnp.float32) * (1.0 / np.sqrt(D))
        Wr = jax.random.normal(ks[3], (E, D), dtype=jnp.float32) * (1.0 / np.sqrt(D))
        A = jax.random.normal(ks[4], (E, R, D), dtype=jnp.float32) * (1.0 / np.sqrt(D))
        Bm = jax.random.normal(ks[5], (O, R), dtype=jnp.float32) * 0.0
        Bm = jnp.broadcast_to(Bm, (E, O, R)) + jax.random.normal(ks[5], (E, O, R), dtype=jnp.float32) * 0.02
        return {'x': x, 'language_ids': language_ids, 'W': W, 'Wr': Wr, 'A': A, 'B': Bm}
    _L1_cond_all = _L1_cond_setup()
    _L1_cond_in = {k: v for k, v in _L1_cond_all.items() if k in ('W', 'Wr', 'A', 'B')}
    del _L1_cond_all
    return {'x': x, 'itok_B_0_23': itok_B_0_23, 'itok_B_0_7': itok_B_0_7, 'L0_cond_W': _L0_cond_in['W'], 'L0_cond_b': _L0_cond_in['b'], 'L0_cond_lora_As': _L0_cond_in['lora_As'], 'L0_cond_lora_Bs': _L0_cond_in['lora_Bs'], 'L1_cond_W': _L1_cond_in['W'], 'L1_cond_Wr': _L1_cond_in['Wr'], 'L1_cond_A': _L1_cond_in['A'], 'L1_cond_B': _L1_cond_in['B']}

def reference(x, itok_B_0_23, itok_B_0_7, L0_cond_W, L0_cond_b, L0_cond_lora_As, L0_cond_lora_Bs, L1_cond_W, L1_cond_Wr, L1_cond_A, L1_cond_B):
    import jax
    import jax.numpy as jnp

    def _L0_cond_ref(x, adapter_mapping, W, b, lora_As, lora_Bs):
        import jax, jax.numpy as jnp
        import numpy as np
        R = 16
        ALPHA = 32
        SCALING = ALPHA / R
        SLOTS = 32
        IN_F = 1024
        OUT_F = 1024
        B, T = (8, 256)
        base_out = jnp.einsum('bti,oi->bto', x, W) + b
        A = lora_As[adapter_mapping]
        Bm = lora_Bs[adapter_mapping]
        lora_h = jnp.einsum('bti,bir->btr', x, A)
        lora_out = jnp.einsum('btr,bro->bto', lora_h, Bm)
        return base_out + lora_out * SCALING

    def _L1_cond_ref(x, language_ids, W, Wr, A, B):
        import jax, jax.numpy as jnp
        import numpy as np
        TOP_K = 2
        LANG_BIAS = 5.0
        SCALING = 32.0 / 16.0
        LANGUAGE_PAD_ID = -1
        base = jnp.einsum('btd,od->bto', x, W)
        E = Wr.shape[0]
        logits = jnp.einsum('btd,ed->bte', x.astype(jnp.float32), Wr.astype(jnp.float32))
        expert_targets = language_ids
        valid = expert_targets >= 0
        tgt = jnp.where(valid, expert_targets, 0)
        bias = jax.nn.one_hot(tgt, E, dtype=logits.dtype) * LANG_BIAS
        bias = jnp.where(valid[:, None], bias, 0.0)
        logits = logits + bias[:, None, :]
        topw, topi = jax.lax.top_k(logits, TOP_K)
        weights = jax.nn.softmax(topw, axis=-1)
        gates = jnp.sum(jax.nn.one_hot(topi, E, dtype=weights.dtype) * weights[..., None], axis=-2)
        gates = gates.astype(x.dtype)
        h = jnp.einsum('btd,erd->bter', x, A)
        lora_out = jnp.einsum('bter,bte,eor->bto', h, gates, B)
        return base + SCALING * lora_out
    x = x + _L0_cond_ref(x, itok_B_0_23, L0_cond_W, L0_cond_b, L0_cond_lora_As, L0_cond_lora_Bs)
    x = x + _L1_cond_ref(x, itok_B_0_7, L1_cond_W, L1_cond_Wr, L1_cond_A, L1_cond_B)
    return x

_drawn_inputs = setup_inputs


def setup_inputs(seed=0):
    import zlib

    import numpy as np

    out = dict(_drawn_inputs(seed))
    spreads = {}
    factors = {'L0_cond_b': 4.211, 'L1_cond_Wr': 3.636}
    for name, (base, spread) in spreads.items():
        noise = np.random.default_rng([zlib.crc32(name.encode()), seed]).standard_normal(out[name].shape)
        drawn = base * np.exp(spread * noise) if base else spread * noise
        out[name] = jnp.asarray(drawn.astype(out[name].dtype))
    for name, factor in factors.items():
        out[name] = (out[name] * factor).astype(out[name].dtype)
    return out
```

```python
from contextlib import ExitStack

import concourse.bass as bass
from concourse import mybir

F32 = mybir.dt.float32
F32R = mybir.dt.float32r
I32 = mybir.dt.int32
U32 = mybir.dt.uint32
ALU = mybir.AluOpType
ACT = mybir.ActivationFunctionType

P = 128
BANK = 512
LANG_BIAS = 5.0
SCALING = 32.0 / 16.0


def build(nc, x, adapter_ids, language_ids, w0, bias0, lora_a0, lora_b0, w1, w_router, lora_a1, lora_b1, out):
    BATCH, SEQ, D = x.shape
    SLOTS, _, R0 = lora_a0.shape
    E, R1, _ = lora_a1.shape
    O = w0.shape[0]
    TILES = BATCH * SEQ // P
    KT = D // P
    OT = O // P
    HALVES = O // BANK
    PER_BANK = BANK // P
    ER = E * R1
    AR = ER + E
    PIECES = 3
    PIECE = (O + 2 * R0) // PIECES
    assert SEQ == 2 * P and O == D and ER == P and HALVES == 2 and KT == 2 * PER_BANK and 4 * R0 == 64 and PIECES * PIECE == O + 2 * R0

    x_rows = x.rearrange("b t d -> (b t) d")
    out_rows = out.rearrange("b t d -> (b t) d")
    a1_rows = lora_a1.rearrange("e r d -> (e r) d")

    ctx = ExitStack()
    with ctx:
        def sb(name, shape, dt=F32):
            return ctx.enter_context(nc.sbuf_tensor(name, shape, dt))

        def pb(name, shape):
            return ctx.enter_context(nc.psum_tensor(name, shape, F32))

        def sem(name):
            return ctx.enter_context(nc.semaphore(name))

        w0_hi, w0_lo = sb("w0_hi", [P, KT, O + 2 * R0], F32R), sb("w0_lo", [P, KT, O], F32R)
        a0 = w0_hi[:, :, O:O + 2 * R0]
        w1_hi, w1_lo = sb("w1_hi", [P, KT, O], F32R), sb("w1_lo", [P, KT, O], F32R)
        ar = sb("ar", [P, KT, 2 * AR], F32R)
        b1_hi, b1_lo = sb("b1_hi", [P, O], F32R), sb("b1_lo", [P, O], F32R)
        a0_raw = sb("a0_raw", [P, KT, R0])
        b0_raw = sb("b0_raw", [P, O])
        b0 = sb("b0", [P, O], F32R)
        x_nat = sb("x_nat", [P, 2, D])
        xT_hi, xT_lo = sb("xT_hi", [P, KT, P], F32R), sb("xT_lo", [P, KT, P], F32R)
        x1_nat = sb("x1_nat", [P, 2, D])
        x1T_hi, x1T_lo = sb("x1T_hi", [P, KT, P], F32R), sb("x1T_lo", [P, KT, P], F32R)
        outs = sb("outs", [P, 2, O])
        stage = sb("stage", [P, 2, D])
        h_part = sb("h_part", [P, R0])
        h_nat = sb("h_nat", [P, R0])
        h_stack = sb("h_stack", [P, 4, 32])
        hT = sb("hT", [P, P], F32R)
        ar_part = sb("ar_part", [P, AR])
        h1_nat = sb("h1_nat", [P, ER])
        routed = sb("routed", [P, E])
        logits = sb("logits", [P, E])
        top = sb("top", [P, 8])
        top_index = sb("top_index", [P, 8], U32)
        top_index_f = sb("top_index_f", [P, 2])
        top_gap = sb("top_gap", [P, 1])
        top_exp = sb("top_exp", [P, 1])
        exp_sum = sb("exp_sum", [P, 1])
        exp_inv = sb("exp_inv", [P, 1])
        top_gate = sb("top_gate", [P, 2])
        gate_each = sb("gate_each", [P, 2, E])
        gates = sb("gates", [P, E])
        gated = sb("gated", [P, ER])
        gT_hi, gT_lo = sb("gT_hi", [P, P], F32R), sb("gT_lo", [P, P], F32R)
        ident = sb("ident", [P, P])
        one = sb("one", [P, 1])
        experts = sb("experts", [P, E])
        languages = sb("languages", [P, BATCH], I32)
        languages_f = sb("languages_f", [P, BATCH])
        language_bias = sb("language_bias", [P, BATCH, E])
        adapters = sb("adapters", [1, BATCH], I32)

        acc0 = pb("acc0", [P, PIECES, BANK])
        h_sum = acc0[:, PIECES - 1, O - (PIECES - 1) * PIECE:PIECE]
        acc1 = pb("acc1", [P, HALVES, BANK])
        turned = pb("turned", [P, 2, BANK])
        ar_bank = pb("ar_bank", [P, BANK])

        ids_in = sem("ids_in")
        languages_in = sem("languages_in")
        bias_in = sem("bias_in")
        x_in = [sem("x_in_even"), sem("x_in_odd")]
        a0_in, b0_in = sem("a0_in"), sem("b0_in")
        stage_in = [sem(f"stage_in{s}") for s in range(5)]
        out_stored = [sem("out_stored_even"), sem("out_stored_odd")]
        ident_made, consts_made, b0_cleared = sem("ident_made"), sem("consts_made"), sem("b0_cleared")
        pool_step, b1_ordered = sem("pool_step"), sem("b1_ordered")
        a0_split, b0_split, bias_split = sem("a0_split"), sem("b0_split"), sem("bias_split")
        w_turned = sem("w_turned")
        x_turned, x1_turned = sem("x_turned"), sem("x1_turned")
        h_summed, h_turned, y0_summed = sem("h_summed"), sem("h_turned"), sem("y0_summed")
        ar_summed, g_turned, y1_summed = sem("ar_summed"), sem("g_turned"), sem("y1_summed")
        w_hi_done, x_hi_done, x1_hi_done = sem("w_hi_done"), sem("x_hi_done"), sem("x1_hi_done")
        h_part_done, hT_done, ar_part_done = sem("h_part_done"), sem("hT_done"), sem("ar_part_done")
        exp_done, g_hi_done = sem("exp_done"), sem("g_hi_done")
        w_lo_done, x_lo_done, x1_lo_done = sem("w_lo_done"), sem("x_lo_done"), sem("x1_lo_done")
        h_stacked, gap_done, gated_done, g_lo_done = sem("h_stacked"), sem("gap_done"), sem("gated_done"), sem("g_lo_done")
        x1_done, out_done = sem("x1_done"), sem("out_done")
        setup_step, h_step, gate_step = sem("setup_step"), sem("h_step"), sem("gate_step")

        slots = [stage[:, 0, :], stage[:, 1, :], x1_nat[:, 1, :], outs[:, 0, :], outs[:, 1, :]]
        loads = ([("w0", t) for t in range(OT)] + [("a1", 0), ("router", 0)]
                 + [("w1", t) for t in range(OT)] + [("b1", 0)])
        jobs = []
        jobs_through = []
        for u, (kind, t) in enumerate(loads):
            for g in range(1 if kind == "router" else 2):
                jobs.append((u, kind, t, g))
            jobs_through.append(len(jobs))
        JOB_BANKS = [acc1[:, 0, :], acc1[:, 1, :], ar_bank[:, :]]
        b1_load = len(loads) - 1
        b1_staged, b1_rows = slots[b1_load % 5], slots[(b1_load + 1) % 5]
        first_job = {(kind, t): jobs_through[u] - (1 if kind == "router" else 2)
                     for u, (kind, t) in enumerate(loads)}
        cut = [first_job["w0", 3], first_job["w0", 6], first_job["a1", 0], first_job["w1", 1],
               first_job["w1", 2], first_job["w1", 3], first_job["w1", 5], first_job["w1", 7], len(jobs)]

        def job_target(j, low):
            u, kind, t, g = jobs[j]
            bank = JOB_BANKS[j % 3]
            four = bank.rearrange("p (k n) -> p k n", k=PER_BANK)
            ks = slice(g * PER_BANK, (g + 1) * PER_BANK)
            if kind == "w0" or kind == "w1":
                w = {"w0": (w0_hi, w0_lo), "w1": (w1_hi, w1_lo)}[kind][low]
                return w[:, ks, t * P:(t + 1) * P], four
            if kind == "a1":
                return ar[:, ks, low * AR:low * AR + ER], four
            if kind == "router":
                return (ar[:, :, low * AR + ER:(low + 1) * AR],
                        bank[:, 0:KT * E].rearrange("p (k n) -> p k n", k=KT))
            b = (b1_hi, b1_lo)[low][:, :].rearrange("q (p j) -> q j p", j=OT)
            return b[:, ks, :], four

        def job_hi(j):
            target, _ = job_target(j, 0)
            return target.bitcast(F32)

        block = ctx.enter_context(nc.Block())

        @block.sync
        def _(sp):
            def load_weights(u):
                kind, t = loads[u]
                if u >= 5:
                    sp.wait_ge(w_turned, jobs_through[u - 5])
                slot = slots[u % 5]
                if kind == "b1":
                    src = lora_b1.rearrange("e (p j) r -> p e (j r)", p=P)
                    dst = slot.rearrange("p (e n) -> p e n", e=E)
                elif kind == "router":
                    src, dst = w_router, slot[0:E, :]
                elif kind == "a1":
                    src, dst = a1_rows, slot
                else:
                    src, dst = {"w0": w0, "w1": w1}[kind][t * P:(t + 1) * P, :], slot
                sp.dma_start(dst, src).then_inc(stage_in[u % 5], 16)

            def load_x(i, slot):
                sp.dma_start(x_nat[:, slot, :], x_rows[bass.ds(i * P, P), :]).then_inc(x_in[slot], 16)

            def load_adapter(b):
                s = sp.value_load(adapters[0:1, bass.ds(b, 1)], min_val=0, max_val=SLOTS - 1)
                sp.dma_start(a0_raw[:, :, :], lora_a0[bass.ds(s, 1), :, :].rearrange("s (k p) r -> p (s k) r", p=P)
                             ).then_inc(a0_in, 16)
                for q in range(4):
                    sp.dma_start(b0_raw[q * R0:(q + 1) * R0, :],
                                 lora_b0[bass.ds(s, 1), :, :].rearrange("s r o -> (s r) o")).then_inc(b0_in, 16)

            def store_out(i, slot):
                sp.wait_ge(out_done, 2 * (i + 1))
                sp.dma_start(out_rows[bass.ds(i * P, P), :], outs[:, slot, :]).then_inc(out_stored[slot], 16)

            sp.dma_start(adapters[0:1, :], adapter_ids.rearrange("(a b) -> a b", a=1)).then_inc(ids_in, 16)
            load_x(0, 0)
            for u in range(4):
                load_weights(u)
            sp.dma_start(languages[:, :], language_ids.rearrange("(a b) -> a b", a=1).to_broadcast([P, BATCH])
                         ).then_inc(languages_in, 16)
            sp.wait_ge(b0_cleared, 1)
            for row in (64, 96):
                sp.dma_start(b0_raw[row:row + 1, :], bias0.rearrange("(a b) -> a b", a=1)).then_inc(bias_in, 16)
            sp.wait_ge(ids_in, 16)
            load_adapter(0)
            load_weights(4)
            for u in range(5, len(loads)):
                load_weights(u)
                if u == OT:
                    load_x(1, 1)
            for slot in range(2):
                sp.sem_inc(out_stored[slot], 16)
            with sp.Fori(1, TILES // 2) as n:
                sp.wait_ge(a0_split, n)
                sp.wait_ge(b0_split, n)
                load_adapter(n)
                for slot in range(2):
                    sp.wait_ge(x1_done, 4 * n + 2 * slot - 2)
                    load_x(2 * n + slot, slot)
                for slot in range(2):
                    store_out(2 * n - 2 + slot, slot)
            for slot in range(2):
                store_out(TILES - 2 + slot, slot)
            for slot in range(2):
                sp.wait_ge(out_stored[slot], 16 * (TILES // 2 + 1))

        @block.gpsimd
        def _(pool):
            steps = [0]

            def link(ins):
                steps[0] += 1
                ins.then_inc(pool_step, 1)
                pool.wait_ge(pool_step, steps[0])

            link(nc.gpsimd.memset(ident[:, :], 0.0))
            nc.gpsimd.affine_select(out=ident[:, :], in_=ident[:, :], compare_op=ALU.not_equal, fill=1.0, base=0,
                                    pattern=[[-1, P]], channel_multiplier=1).then_inc(ident_made, 1)
            pool.wait_ge(ident_made, 1)
            nc.gpsimd.memset(b0_raw[:, :], 0.0).then_inc(b0_cleared, 1)
            pool.wait_ge(b0_cleared, 1)
            link(nc.gpsimd.memset(one[:, :], 1.0))
            link(nc.gpsimd.memset(h_stack[:, :, :], 0.0))
            link(nc.gpsimd.memset(h_stack[:, 2:4, 0:1], 1.0))
            nc.gpsimd.iota(experts[:, :], pattern=[[1, E]], base=0, channel_multiplier=0,
                           allow_small_or_imprecise_dtypes=True).then_inc(consts_made, 1)
            pool.wait_ge(consts_made, 1)

            def split_a0(b, done):
                pool.wait_ge(a0_in, 16 * (b + 1))
                nc.gpsimd.tensor_tensor(out=a0[:, :, 0:R0], in0=a0_raw[:, :, :],
                                        in1=one[:, :].rearrange("p (a b) -> p a b", a=1).to_broadcast([P, KT, R0]),
                                        op=ALU.mult).then_inc(pool_step, 1)
                pool.wait_ge(pool_step, done)
                nc.gpsimd.tensor_tensor(out=a0[:, :, R0:2 * R0], in0=a0_raw[:, :, :],
                                        in1=a0[:, :, 0:R0].bitcast(F32), op=ALU.subtract).then_inc(a0_split, 1)
                pool.wait_ge(a0_split, b + 1)

            def split_b0(b, done):
                pool.wait_ge(b0_in, 64 * (b + 1))
                nc.gpsimd.tensor_tensor(out=b0[0:64, :], in0=b0_raw[0:64, :], in1=one[0:64, :].to_broadcast([64, O]),
                                        op=ALU.mult).then_inc(pool_step, 1)
                pool.wait_ge(pool_step, done)
                nc.gpsimd.tensor_tensor(out=b0[32:64, :], in0=b0_raw[32:64, :],
                                        in1=b0[32:64, :].bitcast(F32), op=ALU.subtract).then_inc(b0_split, 1)
                pool.wait_ge(b0_split, b + 1)

            split_a0(0, steps[0] + 1)
            pool.wait_ge(bias_in, 32)
            nc.gpsimd.tensor_copy(b0[64:128, :], b0_raw[64:128, :]).then_inc(pool_step, 1)
            pool.wait_ge(pool_step, steps[0] + 2)
            nc.gpsimd.tensor_tensor(out=b0[96:128, :], in0=b0_raw[96:128, :],
                                    in1=b0[96:128, :].bitcast(F32), op=ALU.subtract).then_inc(bias_split, 1)
            pool.wait_ge(bias_split, 1)
            split_b0(0, steps[0] + 3)
            pool.wait_ge(stage_in[b1_load % 5], 16 * (b1_load // 5 + 1))
            pool.wait_ge(w_turned, jobs_through[b1_load - 4])
            nc.gpsimd.tensor_copy(b1_rows.rearrange("p (j e r) -> p e j r", j=OT, e=E),
                                  b1_staged.rearrange("p (e j r) -> p e j r", e=E, j=OT)).then_inc(b1_ordered, 1)
            pool.wait_ge(b1_ordered, 1)
            base = steps[0] + 3
            with pool.Fori(1, TILES // 2) as n:
                pool.wait_ge(h_summed, 2 * n)
                split_a0(n, 2 * n + (base - 1))
                pool.wait_ge(y0_summed, PIECES * 2 * n)
                split_b0(n, 2 * n + base)

        @block.tensor
        def _(pe):
            def run_jobs(lo, hi):
                for j in range(lo, hi):
                    u, kind, t, g = jobs[j]
                    if kind == "b1":
                        pe.wait_ge(b1_ordered, 1)
                    else:
                        pe.wait_ge(stage_in[u % 5], 16 * (u // 5 + 1))
                    if j >= 3:
                        pe.wait_ge(w_lo_done, j - 2)
                    bank = JOB_BANKS[j % 3]
                    rows = b1_rows if kind == "b1" else slots[u % 5]
                    if kind == "router":
                        for k in range(KT):
                            last = nc.tensor.transpose(bank[:, k * E:(k + 1) * E], rows[0:E, k * P:(k + 1) * P],
                                                       ident[0:E, 0:E])
                    else:
                        for k in range(PER_BANK):
                            kk = g * PER_BANK + k
                            last = nc.tensor.transpose(bank[:, k * P:(k + 1) * P], rows[:, kk * P:(kk + 1) * P],
                                                       ident[:, :])
                    last.then_inc(w_turned, 1)

            def turn(rows, bank, done):
                for k in range(PER_BANK):
                    last = nc.tensor.transpose(turned[:, bank, k * P:(k + 1) * P],
                                               rows[:, (bank * PER_BANK + k) * P:(bank * PER_BANK + k + 1) * P],
                                               ident[:, :])
                last.then_inc(done, 1)

            def turn_x(i, slot, loads_before, first=False, second=False):
                pe.wait_ge(x_in[slot], 16 * (loads_before + 1))
                if not first:
                    pe.wait_ge(hT_done, i)
                for bank in range(2):
                    if second:
                        pe.wait_ge(x_lo_done, bank + 1)
                    elif not first:
                        pe.wait_ge(x1_lo_done, 2 * i - 3 + bank)
                    turn(x_nat[:, slot, :], bank, x_turned)

            def turn_x1(i, slot, last=False):
                for bank in range(2):
                    pe.wait_ge(x1_done, 2 * i + bank + 1)
                    if last:
                        pe.wait_ge(x_lo_done, 2 * i + bank + 1)
                    else:
                        pe.wait_ge(x_lo_done, 2 * i + bank + 3)
                    turn(x1_nat[:, slot, :], bank, x1_turned)

            def dense(acc, half, hi, lo, w_hi, w_lo):
                cols = slice(half * BANK, (half + 1) * BANK)
                for k in range(KT):
                    nc.tensor.matmul(acc[:, half, :], hi[:, k, :], w_hi[:, k, cols], start=(k == 0), stop=False)
                    nc.tensor.matmul(acc[:, half, :], hi[:, k, :], w_lo[:, k, cols], start=False, stop=False)
                    nc.tensor.matmul(acc[:, half, :], lo[:, k, :], w_hi[:, k, cols], start=False, stop=False)

            def base0(i, piece, side_jobs=(0, 0)):
                lo, hi = side_jobs
                start = piece * PIECE
                low_end = min(start + PIECE, O)
                last_piece = piece == PIECES - 1
                bank = acc0[:, piece, :]
                for k in range(KT):
                    nc.tensor.matmul(bank[:, 0:PIECE], xT_hi[:, k, :], w0_hi[:, k, start:start + PIECE],
                                     start=(k == 0), stop=False)
                    nc.tensor.matmul(bank[:, 0:low_end - start], xT_hi[:, k, :], w0_lo[:, k, start:low_end],
                                     start=False, stop=False)
                    last = nc.tensor.matmul(bank[:, 0:PIECE], xT_lo[:, k, :], w0_hi[:, k, start:start + PIECE],
                                            start=False, stop=last_piece and k == KT - 1)
                    if k < KT - 2:
                        run_jobs(lo + (hi - lo) * k // (KT - 2), lo + (hi - lo) * (k + 1) // (KT - 2))
                if last_piece:
                    last.then_inc(h_summed, 1)

            def tile_ready(i, b):
                pe.wait_ge(x_lo_done, 2 * i + 2)
                pe.wait_ge(x1_done, 2 * i)
                pe.wait_ge(a0_split, b + 1)

            def x1_ar(j):
                pe.wait_ge(x1_lo_done, 2 * j + 2)
                if not (isinstance(j, int) and j == 0):
                    pe.wait_ge(g_lo_done, j)
                for k in range(KT):
                    nc.tensor.matmul(ar_bank[:, 0:2 * AR], x1T_hi[:, k, :], ar[:, k, :], start=(k == 0), stop=False)
                    last = nc.tensor.matmul(ar_bank[:, 0:AR], x1T_lo[:, k, :], ar[:, k, 0:AR], start=False,
                                            stop=(k == KT - 1))
                last.then_inc(ar_summed, 1)

            def base1(j, half):
                if half == 0 and not (isinstance(j, int) and j == 0):
                    pe.wait_ge(out_done, 2 * j)
                dense(acc1, half, x1T_hi, x1T_lo, w1_hi, w1_lo)

            def turn_h(i):
                pe.wait_ge(h_stacked, i + 1)
                nc.tensor.transpose(turned[:, 0, 0:P], h_stack[:, :, :].rearrange("p a b -> p (a b)"),
                                    ident[:, :]).then_inc(h_turned, 1)

            def lora0(i, b):
                pe.wait_ge(hT_done, i + 1)
                pe.wait_ge(b0_split, b + 1)
                pe.wait_ge(bias_split, 1)
                for piece in range(PIECES):
                    start, end = piece * PIECE, min((piece + 1) * PIECE, O)
                    nc.tensor.matmul(acc0[:, piece, 0:end - start], hT[:, :], b0[:, start:end], start=False,
                                     stop=True, skip_group_check=(piece == PIECES - 1)).then_inc(y0_summed, 1)

            def turn_g(j):
                pe.wait_ge(gated_done, j + 1)
                nc.tensor.transpose(ar_bank[:, 0:P], gated[:, :], ident[:, :]).then_inc(g_turned, 1)

            def lora1(j):
                pe.wait_ge(g_lo_done, j + 1)
                for half in range(HALVES):
                    cols = slice(half * BANK, (half + 1) * BANK)
                    nc.tensor.matmul(acc1[:, half, :], gT_hi[:, :], b1_hi[:, cols], start=False, stop=False)
                    nc.tensor.matmul(acc1[:, half, :], gT_hi[:, :], b1_lo[:, cols], start=False, stop=False)
                    nc.tensor.matmul(acc1[:, half, :], gT_lo[:, :], b1_hi[:, cols], start=False,
                                     stop=True).then_inc(y1_summed, 1)

            pe.wait_ge(ident_made, 1)
            turn_x(0, 0, 0, first=True)
            run_jobs(0, cut[0])
            pe.wait_ge(x_lo_done, 2)
            for piece in range(PIECES):
                pe.wait_ge(w_lo_done, cut[piece])
                if piece == PIECES - 1:
                    pe.wait_ge(a0_split, 1)
                base0(0, piece, side_jobs=(cut[piece], cut[piece + 1]))
            run_jobs(cut[3], cut[4])
            turn_h(0)
            turn_x(1, 1, 0, second=True)
            lora0(0, 0)
            run_jobs(cut[4], cut[5])
            tile_ready(1, 0)
            base0(1, 2, side_jobs=(cut[5], cut[6]))
            turn_x1(0, 0)
            base0(1, 0, side_jobs=(cut[6], cut[7]))
            base0(1, 1, side_jobs=(cut[7], cut[8]))
            pe.wait_ge(w_lo_done, cut[8])
            x1_ar(0)
            turn_h(1)
            base1(0, 0)
            lora0(1, 0)
            turn_g(0)
            with pe.Fori(1, TILES // 2) as n:
                for s in range(2):
                    i = 2 * n + s
                    turn_x(i, s, n)
                    base1(i - 2, 1)
                    turn_x1(i - 1, 1 - s)
                    lora1(i - 2)
                    tile_ready(i, n)
                    base0(i, 2)
                    x1_ar(i - 1)
                    base0(i, 0)
                    base0(i, 1)
                    turn_h(i)
                    base1(i - 1, 0)
                    lora0(i, n)
                    turn_g(i - 1)
            base1(TILES - 2, 1)
            turn_x1(TILES - 1, 1, last=True)
            lora1(TILES - 2)
            x1_ar(TILES - 1)
            base1(TILES - 1, 0)
            turn_g(TILES - 1)
            base1(TILES - 1, 1)
            lora1(TILES - 1)

        @block.scalar
        def _(act):
            def copy(dst, src, scale=1.0):
                return nc.scalar.activation(dst, src, ACT.Copy, scale=scale)

            def job_highs(lo, hi):
                for j in range(lo, hi):
                    act.wait_ge(w_turned, j + 1)
                    dst, src = job_target(j, 0)
                    copy(dst, src).then_inc(w_hi_done, 1)

            def highs(i, ready, dst, done):
                for bank in range(2):
                    act.wait_ge(ready, 2 * i + bank + 1)
                    copy(dst[:, bank * PER_BANK:(bank + 1) * PER_BANK, :],
                         turned[:, bank, :].rearrange("p (k n) -> p k n", k=PER_BANK)).then_inc(done, 1)

            def h_low_part(i):
                act.wait_ge(h_summed, i + 1)
                copy(h_part[:, :], h_sum[:, R0:2 * R0], scale=SCALING).then_inc(h_part_done, 1)

            def ar_low_part(j):
                act.wait_ge(ar_summed, j + 1)
                copy(ar_part[:, :], ar_bank[:, AR:2 * AR]).then_inc(ar_part_done, 1)

            def exp_gap(j):
                act.wait_ge(gap_done, j + 1)
                nc.scalar.activation(top_exp[:, :], top_gap[:, :], ACT.Exp).then_inc(exp_done, 1)

            def h_out(i):
                act.wait_ge(h_turned, i + 1)
                copy(hT[:, :], turned[:, 0, 0:P]).then_inc(hT_done, 1)

            def g_high(j):
                act.wait_ge(g_turned, j + 1)
                copy(gT_hi[:, :], ar_bank[:, 0:P]).then_inc(g_hi_done, 1)

            highs(0, x_turned, xT_hi, x_hi_done)
            job_highs(0, cut[3])
            h_low_part(0)
            job_highs(cut[3], cut[4])
            h_out(0)
            highs(1, x_turned, xT_hi, x_hi_done)
            job_highs(cut[4], cut[6])
            h_low_part(1)
            highs(0, x1_turned, x1T_hi, x1_hi_done)
            job_highs(cut[6], cut[8])
            ar_low_part(0)
            exp_gap(0)
            h_out(1)
            g_high(0)
            with act.Fori(1, TILES // 2) as n:
                for s in range(2):
                    i = 2 * n + s
                    highs(i, x_turned, xT_hi, x_hi_done)
                    highs(i - 1, x1_turned, x1T_hi, x1_hi_done)
                    h_low_part(i)
                    ar_low_part(i - 1)
                    exp_gap(i - 1)
                    h_out(i)
                    g_high(i - 1)
            highs(TILES - 1, x1_turned, x1T_hi, x1_hi_done)
            ar_low_part(TILES - 1)
            exp_gap(TILES - 1)
            g_high(TILES - 1)

        @block.vector
        def _(dve):
            def job_lows(lo, hi):
                for j in range(lo, hi):
                    dve.wait_ge(w_hi_done, j + 1)
                    dst, src = job_target(j, 1)
                    nc.vector.tensor_tensor(out=dst, in0=src, in1=job_hi(j), op=ALU.subtract).then_inc(w_lo_done, 1)

            def lows(i, hi_done, hi, lo, done):
                for bank in range(2):
                    ks = slice(bank * PER_BANK, (bank + 1) * PER_BANK)
                    dve.wait_ge(hi_done, 2 * i + bank + 1)
                    nc.vector.tensor_tensor(out=lo[:, ks, :],
                                            in0=turned[:, bank, :].rearrange("p (k n) -> p k n", k=PER_BANK),
                                            in1=hi[:, ks, :].bitcast(F32), op=ALU.subtract).then_inc(done, 1)

            def stack_h(i):
                dve.wait_ge(h_part_done, i + 1)
                nc.vector.scalar_tensor_tensor(out=h_nat[:, :], in0=h_sum[:, 0:R0], scalar=SCALING,
                                               in1=h_part[:, :], op0=ALU.mult, op1=ALU.add).then_inc(h_step, 1)
                twice = h_nat[:, :].rearrange("p (a r) -> p a r", a=1).to_broadcast([P, 2, R0])
                dve.wait_ge(h_step, 2 * i + 1)
                nc.vector.tensor_copy(h_stack[:, 0:2, 0:R0].bitcast(F32R), twice).then_inc(h_step, 1)
                dve.wait_ge(h_step, 2 * i + 2)
                nc.vector.tensor_tensor(out=h_stack[:, 0:2, R0:2 * R0], in0=twice, in1=h_stack[:, 0:2, 0:R0],
                                        op=ALU.subtract).then_inc(h_stacked, 1)

            def set_language_bias():
                dve.wait_ge(languages_in, 16)
                dve.wait_ge(consts_made, 1)
                nc.vector.tensor_copy(languages_f[:, :], languages[:, :]).then_inc(setup_step, 1)
                dve.wait_ge(setup_step, 1)
                nc.vector.tensor_tensor(
                    out=language_bias[:, :, :],
                    in0=experts[:, :].rearrange("p (a e) -> p a e", a=1).to_broadcast([P, BATCH, E]),
                    in1=languages_f[:, :].rearrange("p (b a) -> p b a", a=1).to_broadcast([P, BATCH, E]),
                    op=ALU.is_equal).then_inc(setup_step, 1)
                dve.wait_ge(setup_step, 2)
                nc.vector.tensor_scalar(language_bias[:, :, :], language_bias[:, :, :], LANG_BIAS, None,
                                        ALU.mult).then_inc(setup_step, 1)
                dve.wait_ge(setup_step, 3)

            GATE_STEPS = 13

            def gate(j, b):
                step = [0]

                def mark(ins):
                    step[0] += 1
                    ins.then_inc(gate_step, 1)

                def link(ins):
                    mark(ins)
                    dve.wait_ge(gate_step, GATE_STEPS * j + step[0])

                dve.wait_ge(ar_part_done, j + 1)
                link(nc.vector.tensor_tensor(out=routed[:, :], in0=ar_bank[:, ER:AR], in1=ar_part[:, ER:AR],
                                             op=ALU.add))
                link(nc.vector.tensor_tensor(out=logits[:, :], in0=routed[:, :],
                                             in1=language_bias[:, bass.ds(b, 1), :].rearrange("p a e -> p (a e)"),
                                             op=ALU.add))
                mark(nc.vector.tensor_tensor(out=h1_nat[:, :], in0=ar_bank[:, 0:ER], in1=ar_part[:, 0:ER],
                                             op=ALU.add))
                link(nc.vector.max(out=top[:, :], in_=logits[:, :]))
                nc.vector.tensor_tensor(out=top_gap[:, :], in0=top[:, 1:2], in1=top[:, 0:1],
                                        op=ALU.subtract).then_inc(gap_done, 1)
                link(nc.vector.max_index(out=top_index[:, :], in_max=top[:, :], in_values=logits[:, :]))
                mark(nc.vector.tensor_copy(top_index_f[:, :], top_index[:, 0:2]))
                dve.wait_ge(exp_done, j + 1)
                link(nc.vector.tensor_scalar(exp_sum[:, :], top_exp[:, :], 1.0, None, ALU.add))
                link(nc.vector.reciprocal(exp_inv[:, :], exp_sum[:, :]))
                mark(nc.vector.tensor_scalar(top_gate[:, 0:1], exp_inv[:, :], SCALING, None, ALU.mult))
                link(nc.vector.scalar_tensor_tensor(out=top_gate[:, 1:2], in0=top_exp[:, :], scalar=SCALING,
                                                    in1=exp_inv[:, :], op0=ALU.mult, op1=ALU.mult))
                mark(nc.vector.tensor_scalar(gate_each[:, 0, :], experts[:, :], top_index_f[:, 0:1],
                                             top_gate[:, 0:1], ALU.is_equal, ALU.mult))
                link(nc.vector.tensor_scalar(gate_each[:, 1, :], experts[:, :], top_index_f[:, 1:2],
                                             top_gate[:, 1:2], ALU.is_equal, ALU.mult))
                link(nc.vector.tensor_tensor(out=gates[:, :], in0=gate_each[:, 0, :], in1=gate_each[:, 1, :],
                                             op=ALU.add))
                assert step[0] == GATE_STEPS
                nc.vector.tensor_tensor(
                    out=gated[:, :].rearrange("p (e r) -> p e r", e=E),
                    in0=h1_nat[:, :].rearrange("p (e r) -> p e r", e=E),
                    in1=gates[:, :].rearrange("p (e a) -> p e a", a=1).to_broadcast([P, E, R1]),
                    op=ALU.mult).then_inc(gated_done, 1)

            def residual0(i, slot):
                cols = slice(0, 2 * PIECE)
                dve.wait_ge(y0_summed, 3 * i + 2)
                nc.vector.tensor_tensor(out=x1_nat[:, slot, cols].rearrange("p (c n) -> p c n", c=2),
                                        in0=acc0[:, 0:2, 0:PIECE],
                                        in1=x_nat[:, slot, cols].rearrange("p (c n) -> p c n", c=2),
                                        op=ALU.add).then_inc(x1_done, 1)
                cols = slice(2 * PIECE, O)
                dve.wait_ge(y0_summed, 3 * i + 3)
                nc.vector.tensor_tensor(out=x1_nat[:, slot, cols], in0=acc0[:, 2, 0:O - 2 * PIECE],
                                        in1=x_nat[:, slot, cols], op=ALU.add).then_inc(x1_done, 1)

            def residual1(j, slot, stores_before):
                dve.wait_ge(out_stored[slot], 16 * (stores_before + 1))
                for half in range(HALVES):
                    cols = slice(half * BANK, (half + 1) * BANK)
                    dve.wait_ge(y1_summed, 2 * j + half + 1)
                    nc.vector.tensor_tensor(out=outs[:, slot, cols], in0=acc1[:, half, :],
                                            in1=x1_nat[:, slot, cols], op=ALU.add).then_inc(out_done, 1)

            def g_low(j):
                dve.wait_ge(g_hi_done, j + 1)
                nc.vector.tensor_tensor(out=gT_lo[:, :], in0=ar_bank[:, 0:P], in1=gT_hi[:, :].bitcast(F32),
                                        op=ALU.subtract).then_inc(g_lo_done, 1)

            lows(0, x_hi_done, xT_hi, xT_lo, x_lo_done)
            job_lows(0, cut[3])
            dve.wait_ge(consts_made, 1)
            stack_h(0)
            job_lows(cut[3], cut[4])
            lows(1, x_hi_done, xT_hi, xT_lo, x_lo_done)
            residual0(0, 0)
            job_lows(cut[4], cut[6])
            stack_h(1)
            lows(0, x1_hi_done, x1T_hi, x1T_lo, x1_lo_done)
            set_language_bias()
            job_lows(cut[6], cut[8])
            gate(0, 0)
            residual0(1, 1)
            g_low(0)
            with dve.Fori(1, TILES // 2) as n:
                for s in range(2):
                    i = 2 * n + s
                    lows(i, x_hi_done, xT_hi, xT_lo, x_lo_done)
                    lows(i - 1, x1_hi_done, x1T_hi, x1T_lo, x1_lo_done)
                    residual1(i - 2, s, n - 1)
                    stack_h(i)
                    gate(i - 1, n - 1 + s)
                    residual0(i, s)
                    g_low(i - 1)
            lows(TILES - 1, x1_hi_done, x1T_hi, x1T_lo, x1_lo_done)
            residual1(TILES - 2, 0, TILES // 2 - 1)
            gate(TILES - 1, BATCH - 1)
            g_low(TILES - 1)
            residual1(TILES - 1, 1, TILES // 2 - 1)


_INS = ["x", "itok_B_0_23", "itok_B_0_7", "L0_cond_W", "L0_cond_b", "L0_cond_lora_As", "L0_cond_lora_Bs",
        "L1_cond_W", "L1_cond_Wr", "L1_cond_A", "L1_cond_B"]


def kernel(**inputs):
    import numpy as _np
    import concourse.bacc as _bacc
    from concourse import mybir as _mybir
    from concourse.bass_utils import run_bass_kernel_spmd as _run

    nc = _bacc.Bacc("TRN2", target_bir_lowering=False, num_devices=1)
    arrays, args = {}, []
    for name in _INS:
        a = _np.ascontiguousarray(inputs[name])
        arrays[f"in_{name}"] = a
        args.append(nc.dram_tensor(f"in_{name}", a.shape, _mybir.dt.from_np(a.dtype), kind="ExternalInput").ap())
    shape = inputs["x"].shape
    args.append(nc.dram_tensor("out_y", shape, _mybir.dt.float32, kind="ExternalOutput").ap())
    build(nc, *args)
    r = _run(nc, [arrays], core_ids=[0])
    return r.results[0]["out_y"]
```

```python
from contextlib import ExitStack

import concourse.bass as bass
from concourse import mybir

F32 = mybir.dt.float32
F32R = mybir.dt.float32r
I32 = mybir.dt.int32
U32 = mybir.dt.uint32
ALU = mybir.AluOpType
ACT = mybir.ActivationFunctionType

P = 128
BANK = 512
LANG_BIAS = 5.0
SCALING = 32.0 / 16.0


def build(nc, x, adapter_ids, language_ids, w0, bias0, lora_a0, lora_b0, w1, w_router, lora_a1, lora_b1, out):
    BATCH, SEQ, D = x.shape
    SLOTS, _, R0 = lora_a0.shape
    E, R1, _ = lora_a1.shape
    O = w0.shape[0]
    TILES = BATCH * SEQ // P
    KT = D // P
    OT = O // P
    PER_BANK = BANK // P
    ER = E * R1
    AR = ER + E
    PIECES = 3
    PIECE = (O + 2 * R0) // PIECES
    PIECE1 = 4 * (-(-(O + AR) // (4 * PIECES)))
    assert SEQ == 2 * P and O == D and ER == P and KT == 2 * PER_BANK and 4 * R0 == 64 and PIECES * PIECE == O + 2 * R0
    assert D == 4 * KT * 32 and PIECE % 32 == 0 and (PIECES - 1) * PIECE1 < O and PIECE1 <= BANK

    x_rows = x.rearrange("b t d -> (b t) d")
    out_rows = out.rearrange("b t d -> (b t) d")
    a1_rows = lora_a1.rearrange("e r d -> (e r) d")
    x1_scratch = nc.dram_tensor("x1_scratch", (P, D), F32, kind="Internal").ap()

    ctx = ExitStack()
    with ctx:
        def sb(name, shape, dt=F32):
            return ctx.enter_context(nc.sbuf_tensor(name, shape, dt))

        def pb(name, shape):
            return ctx.enter_context(nc.psum_tensor(name, shape, F32))

        def sem(name):
            return ctx.enter_context(nc.semaphore(name))

        w0_hi, w0_lo = sb("w0_hi", [P, KT, O + 2 * R0], F32R), sb("w0_lo", [P, KT, O], F32R)
        a0 = w0_hi[:, :, O:O + 2 * R0]
        w1_hi, w1_lo = sb("w1_hi", [P, KT, O + AR], F32R), sb("w1_lo", [P, KT, O + AR], F32R)
        b1_hi, b1_lo = sb("b1_hi", [P, O], F32R), sb("b1_lo", [P, O], F32R)
        a0_raw = sb("a0_raw", [P, KT, R0])
        b0_raw = sb("b0_raw", [P, O])
        b0 = sb("b0", [P, O], F32R)
        x_blocks, x_turned_blocks = sb("x_blocks", [P, D]), sb("x_turned_blocks", [P, D])
        xT_hi, xT_lo = sb("xT_hi", [P, KT, P], F32R), sb("xT_lo", [P, KT, P], F32R)
        x1_turned_rows, x1_turned_blocks = sb("x1_turned_rows", [P, D]), sb("x1_turned_blocks", [P, D])
        x1T_hi, x1T_lo = sb("x1T_hi", [P, KT, P], F32R), sb("x1T_lo", [P, KT, P], F32R)
        outs = sb("outs", [P, 2, O])
        stage = sb("stage", [P, 2, D])
        h_part = sb("h_part", [P, R0])
        h_nat = sb("h_nat", [P, R0])
        h_stack = sb("h_stack", [P, 4, 32])
        hT = sb("hT", [P, P], F32R)
        h1_nat = sb("h1_nat", [P, ER])
        logits = sb("logits", [P, E])
        top = sb("top", [P, 8])
        top_index = sb("top_index", [P, 8], U32)
        top_index_f = sb("top_index_f", [P, 2])
        top_gap = sb("top_gap", [P, 1])
        top_exp = sb("top_exp", [P, 1])
        exp_sum = sb("exp_sum", [P, 1])
        exp_inv = sb("exp_inv", [P, 1])
        top_gate = sb("top_gate", [P, 2])
        gate_each = sb("gate_each", [P, 2, E])
        gates = sb("gates", [P, E])
        gated = sb("gated", [P, ER])
        gT_hi, gT_lo = sb("gT_hi", [P, P], F32R), sb("gT_lo", [P, P], F32R)
        ident = sb("ident", [P, P])
        one = sb("one", [P, 1])
        experts = sb("experts", [P, E])
        languages = sb("languages", [P, BATCH], I32)
        languages_f = sb("languages_f", [P, BATCH])
        language_bias = sb("language_bias", [P, BATCH, E])
        adapters = sb("adapters", [1, BATCH], I32)

        acc0 = pb("acc0", [P, PIECES, BANK])
        h_sum = acc0[:, PIECES - 1, O - (PIECES - 1) * PIECE:PIECE]
        acc1 = pb("acc1", [P, PIECES, BANK])
        ar_sum = acc1[:, PIECES - 1, O - (PIECES - 1) * PIECE1:O - (PIECES - 1) * PIECE1 + AR]
        h_bank = pb("h_bank", [P, BANK])
        g_bank = pb("g_bank", [P, BANK])

        ids_in = sem("ids_in")
        languages_in = sem("languages_in")
        bias_in = sem("bias_in")
        x_in = sem("x_in")
        x1_stored, x1_in = sem("x1_stored"), sem("x1_in")
        a0_in, b0_in = sem("a0_in"), sem("b0_in")
        pair_in = [sem("pair_in_stage"), sem("pair_in_outs")]
        single_in = [sem("single_in_even"), sem("single_in_odd")]
        out_stored = [sem("out_stored_even"), sem("out_stored_odd")]
        ident_made, consts_made, b0_cleared = sem("ident_made"), sem("consts_made"), sem("b0_cleared")
        pool_step, b1_ordered = sem("pool_step"), sem("b1_ordered")
        one_added, w_lo_by_pool = sem("one_added"), sem("w_lo_by_pool")
        a0_split, b0_split, bias_split = sem("a0_split"), sem("b0_split"), sem("bias_split")
        b1_turned = sem("b1_turned")
        x0_used, x1_used = sem("x0_used"), sem("x1_used")
        h_summed, h_turned, y0_summed = sem("h_summed"), sem("h_turned"), sem("y0_summed")
        ar_summed, g_turned, y1_summed = sem("ar_summed"), sem("g_turned"), sem("y1_summed")
        w_hi_done, b1_hi_done = sem("w_hi_done"), sem("b1_hi_done")
        x_hi_done, x1_hi_done = sem("x_hi_done"), sem("x1_hi_done")
        h_part_done, hT_done, b0_hi_done = sem("h_part_done"), sem("hT_done"), sem("b0_hi_done")
        exp_done, g_hi_done, out_done = sem("exp_done"), sem("g_hi_done"), sem("out_done")
        w_turned, x_turned, x1_turned = sem("w_turned"), sem("x_turned"), sem("x1_turned")
        w_lo_by_dve, b1_lo_done = sem("w_lo_by_dve"), sem("b1_lo_done")
        x_lo_done, x1_lo_done = sem("x_lo_done"), sem("x1_lo_done")
        h_stacked, gap_done, gated_done, g_lo_done = sem("h_stacked"), sem("gap_done"), sem("gated_done"), sem("g_lo_done")
        setup_step, h_step, gate_step = sem("setup_step"), sem("h_step"), sem("gate_step")

        loads = ([("w0", t) for t in (6, 7, 5, 4, 3, 2, 1, 0)] + [("a1", 0)] + [("w1", t) for t in range(OT - 2, OT)]
                 + [("router", 0)] + [("w1", t) for t in range(OT - 2)])
        B1_LOAD = len(loads)
        x1_buffers = [x1_turned_rows[:, :], x1_turned_blocks[:, :]]

        def raw_slot(u):
            if 2 <= u < OT:
                return (stage, outs)[u // 2 % 2][:, 1 - u % 2, :]
            return stage[:, u % 2, :]

        def turned_slot(u):
            return x1_buffers[u % 2] if u < OT else outs[:, u % 2, :]

        def wait_raw_free(engine, u):
            if u < OT:
                if u >= 4:
                    engine.wait_ge(w_turned, u - 2)
            else:
                engine.wait_ge(w_turned, OT - 2 if u < OT + 2 else u - 1)

        def wait_raw(engine, u):
            if u < 2:
                engine.wait_ge(single_in[u], 64)
            elif u < OT:
                engine.wait_ge(pair_in[u // 2 % 2], 64 * (u // 4 + (u // 2 % 2)))
            else:
                before = 1 + (u - OT) // 2
                engine.wait_ge(single_in[u % 2], 64 * before + (16 if u == B1_LOAD else 64))

        def wait_turned_free(engine, u):
            if OT <= u < OT + 2:
                engine.wait_ge(w_turned, OT)
            elif u >= 2:
                wait_split(engine, u - 1)

        def gets_one(u):
            return loads[u][0] in ("w0", "w1")

        def additions(u):
            return len([v for v in range(u + 1) if gets_one(v)])

        def loaded_through(names):
            return 1 + max(u for u, load in enumerate(loads) if load in names)

        pool_lows = (3, 6, 9, 12, 14, 16)

        def wait_split(engine, count):
            by_pool = len([u for u in range(count) if u in pool_lows])
            if count > by_pool:
                engine.wait_ge(w_lo_by_dve, count - by_pool)
            if by_pool:
                engine.wait_ge(w_lo_by_pool, by_pool)

        H0_AT, H1_AT, X1L_AT = OT - 3, OT + 2, OT + 5
        LATE = (OT + 6,)
        assert H0_AT < OT <= H1_AT < X1L_AT < B1_LOAD

        b1_staged, b1_rows = raw_slot(B1_LOAD), turned_slot(B1_LOAD)

        def in_place(blocks, ks=slice(0, KT)):
            return blocks.rearrange("p (b k j) -> p b k j", b=4, k=KT)[:, :, ks, :]

        def chunks(target, ks=slice(0, KT)):
            return target[:, ks, :].rearrange("p k (b j) -> p b k j", b=4)

        def weight_target(u, w):
            kind, t = loads[u]
            turned = turned_slot(u)
            if kind == "router":
                return w[1][:, :, O + ER:O + AR], turned[:, 0:KT * 32].rearrange("p (k j) -> p k j", k=KT)[:, :, 0:E]
            start = {"w0": t * P, "w1": t * P, "a1": O}[kind]
            return chunks(w[kind != "w0"][:, :, start:start + P]), in_place(turned)

        def b1_target(b1, g):
            return b1[:, :].rearrange("q (p j) -> q j p", j=OT)[:, g * PER_BANK:(g + 1) * PER_BANK, :]

        def b1_bank(g):
            return (h_bank, g_bank)[g][:, :].rearrange("p (k n) -> p k n", k=PER_BANK)

        block = ctx.enter_context(nc.Block())

        @block.sync
        def _(sp):
            def load_blocks(dst, src, arrived):
                for a in range(4):
                    sp.dma_start(dst[32 * a:32 * a + 32, :].rearrange("j (b n) -> j b n", b=4),
                                 src[:, D // 4 * a:D // 4 * (a + 1)].rearrange("(b j) n -> j b n", b=4)
                                 ).then_inc(arrived, 16)

            def load_weights(u):
                wait_raw_free(sp, u)
                slot = raw_slot(u)
                arrived = single_in[u % 2]
                if u == B1_LOAD:
                    sp.dma_start(slot.rearrange("p (e n) -> p e n", e=E),
                                 lora_b1.rearrange("e (p j) r -> p e (j r)", p=P)).then_inc(arrived, 16)
                    return
                kind, t = loads[u]
                if kind == "router":
                    for a in range(4):
                        sp.dma_start(slot[32 * a:32 * a + E, 0:D // 4], w_router[:, D // 4 * a:D // 4 * (a + 1)]
                                     ).then_inc(arrived, 16)
                else:
                    rows = {"w0": w0, "w1": w1, "a1": a1_rows}[kind]
                    load_blocks(slot, rows[t * P:(t + 1) * P, :], arrived)

            def load_pair(u):
                wait_raw_free(sp, u)
                t = loads[u + 1][1]
                pair = (stage, outs)[u // 2 % 2]
                for a in range(4):
                    sp.dma_start(pair[32 * a:32 * a + 32, :, :].rearrange("j s (b n) -> j (s b) n", b=4),
                                 w0[t * P:(t + 2) * P, D // 4 * a:D // 4 * (a + 1)].rearrange(
                                     "(b j) n -> j b n", b=8)).then_inc(pair_in[u // 2 % 2], 16)

            def load_x(i):
                load_blocks(x_blocks[:, :], x_rows[bass.ds(i * P, P), :], x_in)

            def store_x1(i):
                sp.wait_ge(x1_turned, 2 * i + 2)
                sp.dma_start(x1_scratch, x1_turned_rows[:, :]).then_inc(x1_stored, 16)

            def place_x1(i):
                sp.wait_ge(x1_stored, 16 * (i + 1))
                load_blocks(x1_turned_blocks[:, :], x1_scratch, x1_in)

            def slot_id(b):
                return sp.value_load(adapters[0:1, bass.ds(b, 1)], min_val=0, max_val=SLOTS - 1)

            def load_a0(s):
                for a in range(4):
                    sp.dma_start(a0_raw[32 * a:32 * a + 32, :, :],
                                 lora_a0[bass.ds(s, 1), D // 4 * a:D // 4 * (a + 1), :].rearrange(
                                     "s (k c) r -> c (s k) r", k=KT)).then_inc(a0_in, 16)

            def load_b0(s):
                for q in range(4):
                    sp.dma_start(b0_raw[q * R0:(q + 1) * R0, :],
                                 lora_b0[bass.ds(s, 1), :, :].rearrange("s r o -> (s r) o")).then_inc(b0_in, 16)

            def store_out(i, slot):
                sp.wait_ge(out_done, 2 * (i + 1))
                sp.dma_start(out_rows[bass.ds(i * P, P), :], outs[:, slot, :]).then_inc(out_stored[slot], 16)

            sp.dma_start(adapters[0:1, :], adapter_ids.rearrange("(a b) -> a b", a=1)).then_inc(ids_in, 16)
            load_x(0)
            for u in range(2):
                load_weights(u)
            sp.wait_ge(ids_in, 16)
            first_id = slot_id(0)
            load_pair(2)
            load_a0(first_id)
            sp.wait_ge(b0_cleared, 1)
            load_b0(first_id)
            for row in (64, 96):
                sp.dma_start(b0_raw[row:row + 1, :], bias0.rearrange("(a b) -> a b", a=1)).then_inc(bias_in, 16)
            load_pair(4)
            load_pair(6)
            sp.dma_start(languages[:, :], language_ids.rearrange("(a b) -> a b", a=1).to_broadcast([P, BATCH])
                         ).then_inc(languages_in, 16)
            sp.wait_ge(x_turned, 1)
            load_x(1)
            for u in range(OT, OT + 4):
                load_weights(u)
            store_x1(0)
            for u in range(OT + 4, OT + 6):
                load_weights(u)
            wait_split(sp, OT)
            place_x1(0)
            for u in range(OT + 6, B1_LOAD + 1):
                load_weights(u)
            for slot in range(2):
                sp.sem_inc(out_stored[slot], 16)
            with sp.Fori(1, TILES // 2) as n:
                s = slot_id(n)
                sp.wait_ge(a0_split, n)
                load_a0(s)
                sp.wait_ge(b0_split, n)
                load_b0(s)
                for slot in range(2):
                    i = 2 * n + slot
                    sp.wait_ge(x_turned, i)
                    load_x(i)
                    store_x1(i - 1)
                    place_x1(i - 1)
                    store_out(i - 2, slot)
            store_x1(TILES - 1)
            place_x1(TILES - 1)
            for slot in range(2):
                store_out(TILES - 2 + slot, slot)
            for slot in range(2):
                sp.wait_ge(out_stored[slot], 16 * (TILES // 2 + 1))

        @block.gpsimd
        def _(pool):
            steps = [0]

            def link(ins):
                steps[0] += 1
                ins.then_inc(pool_step, 1)
                pool.wait_ge(pool_step, steps[0])

            link(nc.gpsimd.memset(ident[:, :], 0.0))
            nc.gpsimd.affine_select(out=ident[:, :], in_=ident[:, :], compare_op=ALU.not_equal, fill=1.0, base=0,
                                    pattern=[[-1, P]], channel_multiplier=1).then_inc(ident_made, 1)
            pool.wait_ge(ident_made, 1)
            nc.gpsimd.memset(b0_raw[:, :], 0.0).then_inc(b0_cleared, 1)
            pool.wait_ge(b0_cleared, 1)
            link(nc.gpsimd.memset(one[:, :], 1.0))
            link(nc.gpsimd.memset(h_stack[:, :, :], 0.0))
            link(nc.gpsimd.memset(h_stack[:, 2:4, 0:1], 1.0))
            nc.gpsimd.iota(experts[:, :], pattern=[[1, E]], base=0, channel_multiplier=0,
                           allow_small_or_imprecise_dtypes=True).then_inc(consts_made, 1)
            pool.wait_ge(consts_made, 1)

            def split_a0(b, done):
                pool.wait_ge(a0_in, 64 * (b + 1))
                nc.gpsimd.tensor_tensor(out=a0[:, :, 0:R0], in0=a0_raw[:, :, :],
                                        in1=one[:, :].rearrange("p (a b) -> p a b", a=1).to_broadcast([P, KT, R0]),
                                        op=ALU.mult).then_inc(pool_step, 1)
                pool.wait_ge(pool_step, done)
                nc.gpsimd.tensor_tensor(out=a0[:, :, R0:2 * R0], in0=a0_raw[:, :, :],
                                        in1=a0[:, :, 0:R0].bitcast(F32), op=ALU.subtract).then_inc(a0_split, 1)
                pool.wait_ge(a0_split, b + 1)

            def high_b0(b, done):
                pool.wait_ge(b0_in, 64 * (b + 1))
                nc.gpsimd.tensor_tensor(out=b0[0:64, :], in0=b0_raw[0:64, :], in1=one[0:64, :].to_broadcast([64, O]),
                                        op=ALU.mult).then_inc(pool_step, 1)
                pool.wait_ge(pool_step, done)

            def low_b0(b):
                nc.gpsimd.tensor_tensor(out=b0[32:64, :], in0=b0_raw[32:64, :],
                                        in1=b0[32:64, :].bitcast(F32), op=ALU.subtract).then_inc(b0_split, 1)
                pool.wait_ge(b0_split, b + 1)

            def x_low(i):
                for bank in range(2):
                    ks = slice(bank * PER_BANK, (bank + 1) * PER_BANK)
                    pool.wait_ge(x_hi_done, 2 * i + bank + 1)
                    nc.gpsimd.tensor_tensor(out=chunks(xT_lo, ks), in0=in_place(x_turned_blocks[:, :], ks),
                                            in1=chunks(xT_hi, ks).bitcast(F32), op=ALU.subtract).then_inc(x_lo_done, 1)
                    pool.wait_ge(x_lo_done, 2 * i + bank + 1)

            def add_one(u):
                t = loads[u][1]
                wait_raw(pool, u)
                group = slice(32 * (t // 2), 32 * (t // 2) + 32)
                first = raw_slot(u)[group, 128 * (t % 2):128 * (t % 2) + 32]
                diagonal = bass.AP(tensor=first.tensor, offset=first.offset,
                                   ap=[list(first.ap[0]), [D // 4 + 32, 4], [1, 32]])
                ones = ident[group, group].rearrange("p (a n) -> p a n", a=1).to_broadcast([32, 4, 32])
                nc.gpsimd.tensor_tensor(out=diagonal, in0=diagonal, in1=ones, op=ALU.add).then_inc(one_added, 1)
                pool.wait_ge(one_added, additions(u))

            def low_weights(u):
                pool.wait_ge(w_hi_done, u + 1)
                lo, src = weight_target(u, (w0_lo, w1_lo))
                hi, _ = weight_target(u, (w0_hi, w1_hi))
                nc.gpsimd.tensor_tensor(out=lo, in0=src, in1=hi.bitcast(F32), op=ALU.subtract).then_inc(w_lo_by_pool, 1)
                pool.wait_ge(w_lo_by_pool, len([v for v in pool_lows if v <= u]))

            add_one(0)
            add_one(1)
            add_one(2)
            add_one(3)
            split_a0(0, steps[0] + 1)
            low_weights(3)
            add_one(4)
            add_one(5)
            pool.wait_ge(b0_hi_done, 1)
            low_b0(0)
            add_one(6)
            add_one(7)
            low_weights(6)
            nc.gpsimd.tensor_tensor(out=b0[96:128, :], in0=b0_raw[96:128, :],
                                    in1=b0[96:128, :].bitcast(F32), op=ALU.subtract).then_inc(bias_split, 1)
            pool.wait_ge(bias_split, 1)
            for u in range(OT, B1_LOAD):
                if gets_one(u):
                    add_one(u)
                if u - 1 in pool_lows:
                    low_weights(u - 1)
            wait_raw(pool, B1_LOAD)
            wait_turned_free(pool, B1_LOAD)
            nc.gpsimd.tensor_copy(b1_rows.rearrange("p (j e r) -> p e j r", j=OT, e=E),
                                  b1_staged.rearrange("p (e j r) -> p e j r", e=E, j=OT)).then_inc(b1_ordered, 1)
            pool.wait_ge(b1_ordered, 1)
            base = steps[0] + 1
            with pool.Fori(1, TILES // 2) as n:
                pool.wait_ge(h_summed, 2 * n)
                split_a0(n, 2 * n + (base - 1))
                x_low(2 * n)
                pool.wait_ge(y0_summed, PIECES * 2 * n)
                high_b0(n, 2 * n + base)
                low_b0(n)
                x_low(2 * n + 1)

        @block.tensor
        def _(pe):
            def turn_b1():
                pe.wait_ge(b1_ordered, 1)
                for g in range(2):
                    for k in range(PER_BANK):
                        j = g * PER_BANK + k
                        last = nc.tensor.transpose(b1_bank(g)[:, k, :], b1_rows[:, j * P:(j + 1) * P], ident[:, :])
                    last.then_inc(b1_turned, 1)

            def base0(i, piece, end_of_tile=1):
                start = piece * PIECE
                low_end = min(start + PIECE, O)
                last_piece = piece == PIECES - 1
                bank = acc0[:, piece, :]
                for k in range(KT):
                    nc.tensor.matmul(bank[:, 0:PIECE], xT_hi[:, k, :], w0_hi[:, k, start:start + PIECE],
                                     start=(k == 0), stop=False)
                    nc.tensor.matmul(bank[:, 0:low_end - start], xT_hi[:, k, :], w0_lo[:, k, start:low_end],
                                     start=False, stop=False)
                    last = nc.tensor.matmul(bank[:, 0:PIECE], xT_lo[:, k, :], w0_hi[:, k, start:start + PIECE],
                                            start=False, stop=last_piece and k == KT - 1)
                if last_piece:
                    last.then_inc(h_summed, 1)
                if piece == end_of_tile:
                    last.then_inc(x0_used, 1)

            def tile_ready(i, b):
                pe.wait_ge(x_lo_done, 2 * i + 2)
                pe.wait_ge(x1_turned, 2 * i)
                pe.wait_ge(a0_split, b + 1)

            def base1(j, piece):
                last_piece = piece == PIECES - 1
                if last_piece:
                    pe.wait_ge(x1_lo_done, 2 * j + 2)
                    if not (isinstance(j, int) and j == 0):
                        pe.wait_ge(out_done, 2 * j)
                start, end = piece * PIECE1, min((piece + 1) * PIECE1, O + AR)
                for k in range(KT):
                    for x_part, w_part in ((x1T_hi, w1_hi), (x1T_hi, w1_lo), (x1T_lo, w1_hi)):
                        final = k == KT - 1 and x_part is x1T_lo
                        last = nc.tensor.matmul(acc1[:, piece, 0:end - start], x_part[:, k, :],
                                                w_part[:, k, start:end], start=(k == 0 and w_part is w1_hi and x_part is x1T_hi),
                                                stop=last_piece and final)
                if last_piece:
                    last.then_inc(ar_summed, 1)
                if piece == 1:
                    last.then_inc(x1_used, 1)

            def turn_h(i):
                pe.wait_ge(h_stacked, i + 1)
                nc.tensor.transpose(h_bank[:, 0:P], h_stack[:, :, :].rearrange("p a b -> p (a b)"),
                                    ident[:, :]).then_inc(h_turned, 1)

            def lora0(i, b):
                pe.wait_ge(hT_done, i + 1)
                pe.wait_ge(b0_split, b + 1)
                pe.wait_ge(bias_split, 1)
                for piece in (PIECES - 1, 0, 1):
                    start, end = piece * PIECE, min((piece + 1) * PIECE, O)
                    nc.tensor.matmul(acc0[:, piece, 0:end - start], hT[:, :], b0[:, start:end], start=False,
                                     stop=True, skip_group_check=(piece == PIECES - 1)).then_inc(y0_summed, 1)

            def turn_g(j):
                pe.wait_ge(gated_done, j + 1)
                nc.tensor.transpose(g_bank[:, 0:P], gated[:, :], ident[:, :]).then_inc(g_turned, 1)

            def lora1(j):
                pe.wait_ge(g_lo_done, j + 1)
                for piece in (PIECES - 1, 0, 1):
                    start, end = piece * PIECE1, min((piece + 1) * PIECE1, O)
                    for g_part, b_part in ((gT_hi, b1_hi), (gT_hi, b1_lo), (gT_lo, b1_hi)):
                        final = g_part is gT_lo
                        last = nc.tensor.matmul(acc1[:, piece, 0:end - start], g_part[:, :], b_part[:, start:end],
                                                start=False, stop=final, skip_group_check=(piece == PIECES - 1))
                    last.then_inc(y1_summed, 1)

            pe.wait_ge(ident_made, 1)
            pe.wait_ge(x_lo_done, 2)
            pe.wait_ge(a0_split, 1)
            for piece in (2, 1, 0):
                tiles = range(piece * PIECE // P, min((piece + 1) * PIECE - 1, O - 1) // P + 1)
                wait_split(pe, loaded_through([("w0", t) for t in tiles]))
                base0(0, piece, end_of_tile=0)
                if piece == 1:
                    turn_h(0)
            lora0(0, 0)
            tile_ready(1, 0)
            base0(1, 2)
            base0(1, 0)
            turn_h(1)
            base0(1, 1)
            lora0(1, 0)
            for piece in (2, 0, 1):
                tiles = range(piece * PIECE1 // P, min((piece + 1) * PIECE1 - 1, O - 1) // P + 1)
                wait_split(pe, loaded_through([("w1", t) for t in tiles] + [("a1", 0), ("router", 0)]))
                base1(0, piece)
                if piece == 0:
                    turn_b1()
            pe.wait_ge(b1_lo_done, 2)
            turn_g(0)
            with pe.Fori(1, TILES // 2) as n:
                for s in range(2):
                    i = 2 * n + s
                    tile_ready(i, n)
                    base0(i, 2)
                    lora1(i - 2)
                    base0(i, 0)
                    turn_h(i)
                    base0(i, 1)
                    lora0(i, n)
                    base1(i - 1, 2)
                    base1(i - 1, 0)
                    base1(i - 1, 1)
                    turn_g(i - 1)
            lora1(TILES - 2)
            base1(TILES - 1, 2)
            base1(TILES - 1, 0)
            base1(TILES - 1, 1)
            turn_g(TILES - 1)
            lora1(TILES - 1)

        @block.scalar
        def _(act):
            def copy(dst, src, scale=1.0):
                return nc.scalar.activation(dst, src, ACT.Copy, scale=scale)

            def high_weights(lo, hi):
                for u in range(lo, hi):
                    act.wait_ge(w_turned, u + 1)
                    dst, src = weight_target(u, (w0_hi, w1_hi))
                    copy(dst, src).then_inc(w_hi_done, 1)

            def b1_highs():
                for g in range(2):
                    act.wait_ge(b1_turned, g + 1)
                    copy(b1_target(b1_hi, g), b1_bank(g)).then_inc(b1_hi_done, 1)

            def x_highs(i):
                act.wait_ge(x_turned, i + 1)
                if not (isinstance(i, int) and i == 0):
                    act.wait_ge(x0_used, i)
                for bank in range(2):
                    ks = slice(bank * PER_BANK, (bank + 1) * PER_BANK)
                    copy(chunks(xT_hi, ks), in_place(x_turned_blocks[:, :], ks)).then_inc(x_hi_done, 1)

            def x1_highs(i):
                act.wait_ge(x1_in, 64 * (i + 1))
                if not (isinstance(i, int) and i == 0):
                    act.wait_ge(x1_used, i)
                for bank in range(2):
                    ks = slice(bank * PER_BANK, (bank + 1) * PER_BANK)
                    copy(chunks(x1T_hi, ks), in_place(x1_turned_blocks[:, :], ks)).then_inc(x1_hi_done, 1)

            def y_out(j, slot, stores_before):
                act.wait_ge(out_stored[slot], 16 * (stores_before + 1))
                cols = slice((PIECES - 1) * PIECE1, O)
                act.wait_ge(y1_summed, 3 * j + 1)
                copy(outs[:, slot, cols], acc1[:, PIECES - 1, 0:O - (PIECES - 1) * PIECE1]).then_inc(out_done, 1)
                cols = slice(0, 2 * PIECE1)
                act.wait_ge(y1_summed, 3 * j + 3)
                copy(outs[:, slot, cols].rearrange("p (c n) -> p c n", c=2), acc1[:, 0:2, 0:PIECE1]
                     ).then_inc(out_done, 1)

            def h_low_part(i):
                act.wait_ge(h_summed, i + 1)
                copy(h_part[:, :], h_sum[:, R0:2 * R0], scale=SCALING).then_inc(h_part_done, 1)

            def exp_gap(j):
                act.wait_ge(gap_done, j + 1)
                nc.scalar.activation(top_exp[:, :], top_gap[:, :], ACT.Exp).then_inc(exp_done, 1)

            def h_out(i):
                act.wait_ge(h_turned, i + 1)
                copy(hT[:, :], h_bank[:, 0:P]).then_inc(hT_done, 1)

            def g_high(j):
                act.wait_ge(g_turned, j + 1)
                copy(gT_hi[:, :], g_bank[:, 0:P]).then_inc(g_hi_done, 1)

            x_highs(0)
            high_weights(0, 4)
            act.wait_ge(b0_in, 64)
            act.wait_ge(bias_in, 32)
            copy(b0[:, :], b0_raw[:, :]).then_inc(b0_hi_done, 1)
            high_weights(4, H0_AT + 1)
            h_low_part(0)
            high_weights(H0_AT + 1, OT)
            h_out(0)
            high_weights(OT, OT + 1)
            x_highs(1)
            high_weights(OT + 1, H1_AT + 1)
            h_low_part(1)
            high_weights(H1_AT + 1, X1L_AT - 1)
            h_out(1)
            high_weights(X1L_AT - 1, X1L_AT + 1)
            x1_highs(0)
            high_weights(X1L_AT + 1, B1_LOAD)
            b1_highs()
            with act.Fori(1, TILES // 2) as n:
                for s in range(2):
                    i = 2 * n + s
                    x_highs(i)
                    exp_gap(i - 2)
                    g_high(i - 2)
                    h_low_part(i)
                    x1_highs(i - 1)
                    y_out(i - 2, s, n - 1)
                    h_out(i)
            exp_gap(TILES - 2)
            g_high(TILES - 2)
            x1_highs(TILES - 1)
            y_out(TILES - 2, 0, TILES // 2 - 1)
            exp_gap(TILES - 1)
            g_high(TILES - 1)
            y_out(TILES - 1, 1, TILES // 2 - 1)

        @block.vector
        def _(dve):
            def turn_weights(u):
                if gets_one(u):
                    dve.wait_ge(one_added, additions(u))
                else:
                    wait_raw(dve, u)
                wait_turned_free(dve, u)
                size = KT * 32 if loads[u][0] == "router" else D
                nc.vector.transpose(turned_slot(u)[:, 0:size], raw_slot(u)[:, 0:size]
                                    ).then_inc(w_turned, 1)

            def low_weights(u):
                if u in pool_lows:
                    return
                dve.wait_ge(w_hi_done, u + 1)
                lo, src = weight_target(u, (w0_lo, w1_lo))
                hi, _ = weight_target(u, (w0_hi, w1_hi))
                nc.vector.tensor_tensor(out=lo, in0=src, in1=hi.bitcast(F32), op=ALU.subtract).then_inc(w_lo_by_dve, 1)

            def weights(lo, hi):
                for u in range(lo, hi):
                    if u + 1 < B1_LOAD and u + 1 not in LATE:
                        turn_weights(u + 1)
                    low_weights(u)

            def x_lows(i):
                for bank in range(2):
                    ks = slice(bank * PER_BANK, (bank + 1) * PER_BANK)
                    dve.wait_ge(x_hi_done, 2 * i + bank + 1)
                    nc.vector.tensor_tensor(out=chunks(xT_lo, ks), in0=in_place(x_turned_blocks[:, :], ks),
                                            in1=chunks(xT_hi, ks).bitcast(F32), op=ALU.subtract).then_inc(x_lo_done, 1)

            def b1_lows():
                for g in range(2):
                    dve.wait_ge(b1_hi_done, g + 1)
                    nc.vector.tensor_tensor(out=b1_target(b1_lo, g), in0=b1_bank(g),
                                            in1=b1_target(b1_hi, g).bitcast(F32), op=ALU.subtract
                                            ).then_inc(b1_lo_done, 1)

            def x1_lows(i):
                for bank in range(2):
                    ks = slice(bank * PER_BANK, (bank + 1) * PER_BANK)
                    dve.wait_ge(x1_hi_done, 2 * i + bank + 1)
                    nc.vector.tensor_tensor(out=chunks(x1T_lo, ks), in0=in_place(x1_turned_blocks[:, :], ks),
                                            in1=chunks(x1T_hi, ks).bitcast(F32), op=ALU.subtract
                                            ).then_inc(x1_lo_done, 1)

            def stack_h(i):
                dve.wait_ge(h_part_done, i + 1)
                nc.vector.scalar_tensor_tensor(out=h_nat[:, :], in0=h_sum[:, 0:R0], scalar=SCALING,
                                               in1=h_part[:, :], op0=ALU.mult, op1=ALU.add).then_inc(h_step, 1)
                twice = h_nat[:, :].rearrange("p (a r) -> p a r", a=1).to_broadcast([P, 2, R0])
                dve.wait_ge(h_step, 2 * i + 1)
                nc.vector.tensor_copy(h_stack[:, 0:2, 0:R0].bitcast(F32R), twice).then_inc(h_step, 1)
                dve.wait_ge(h_step, 2 * i + 2)
                nc.vector.tensor_tensor(out=h_stack[:, 0:2, R0:2 * R0], in0=twice, in1=h_stack[:, 0:2, 0:R0],
                                        op=ALU.subtract).then_inc(h_stacked, 1)

            def set_language_bias():
                dve.wait_ge(languages_in, 16)
                dve.wait_ge(consts_made, 1)
                nc.vector.tensor_copy(languages_f[:, :], languages[:, :]).then_inc(setup_step, 1)
                dve.wait_ge(setup_step, 1)
                nc.vector.tensor_tensor(
                    out=language_bias[:, :, :],
                    in0=experts[:, :].rearrange("p (a e) -> p a e", a=1).to_broadcast([P, BATCH, E]),
                    in1=languages_f[:, :].rearrange("p (b a) -> p b a", a=1).to_broadcast([P, BATCH, E]),
                    op=ALU.is_equal).then_inc(setup_step, 1)
                dve.wait_ge(setup_step, 2)
                nc.vector.tensor_scalar(language_bias[:, :, :], language_bias[:, :, :], LANG_BIAS, None,
                                        ALU.mult).then_inc(setup_step, 1)
                dve.wait_ge(setup_step, 3)

            GATE_STEPS = 12

            def gate(j, b):
                step = [0]

                def mark(ins):
                    step[0] += 1
                    ins.then_inc(gate_step, 1)

                def link(ins):
                    mark(ins)
                    dve.wait_ge(gate_step, GATE_STEPS * j + step[0])

                dve.wait_ge(ar_summed, j + 1)
                link(nc.vector.tensor_tensor(out=logits[:, :], in0=ar_sum[:, ER:AR],
                                             in1=language_bias[:, bass.ds(b, 1), :].rearrange("p a e -> p (a e)"),
                                             op=ALU.add))
                mark(nc.vector.tensor_copy(h1_nat[:, :], ar_sum[:, 0:ER]))
                link(nc.vector.max(out=top[:, :], in_=logits[:, :]))
                nc.vector.tensor_tensor(out=top_gap[:, :], in0=top[:, 1:2], in1=top[:, 0:1],
                                        op=ALU.subtract).then_inc(gap_done, 1)
                link(nc.vector.max_index(out=top_index[:, :], in_max=top[:, :], in_values=logits[:, :]))
                mark(nc.vector.tensor_copy(top_index_f[:, :], top_index[:, 0:2]))
                dve.wait_ge(exp_done, j + 1)
                link(nc.vector.tensor_scalar(exp_sum[:, :], top_exp[:, :], 1.0, None, ALU.add))
                link(nc.vector.reciprocal(exp_inv[:, :], exp_sum[:, :]))
                mark(nc.vector.tensor_scalar(top_gate[:, 0:1], exp_inv[:, :], SCALING, None, ALU.mult))
                link(nc.vector.scalar_tensor_tensor(out=top_gate[:, 1:2], in0=top_exp[:, :], scalar=SCALING,
                                                    in1=exp_inv[:, :], op0=ALU.mult, op1=ALU.mult))
                mark(nc.vector.tensor_scalar(gate_each[:, 0, :], experts[:, :], top_index_f[:, 0:1],
                                             top_gate[:, 0:1], ALU.is_equal, ALU.mult))
                link(nc.vector.tensor_scalar(gate_each[:, 1, :], experts[:, :], top_index_f[:, 1:2],
                                             top_gate[:, 1:2], ALU.is_equal, ALU.mult))
                link(nc.vector.tensor_tensor(out=gates[:, :], in0=gate_each[:, 0, :], in1=gate_each[:, 1, :],
                                             op=ALU.add))
                assert step[0] == GATE_STEPS
                nc.vector.tensor_tensor(
                    out=gated[:, :].rearrange("p (e r) -> p e r", e=E),
                    in0=h1_nat[:, :].rearrange("p (e r) -> p e r", e=E),
                    in1=gates[:, :].rearrange("p (e a) -> p e a", a=1).to_broadcast([P, E, R1]),
                    op=ALU.mult).then_inc(gated_done, 1)

            def turn_x(i):
                dve.wait_ge(x_in, 64 * (i + 1))
                if not (isinstance(i, int) and i == 0):
                    dve.wait_ge(x_lo_done, 2 * i)
                nc.vector.transpose(x_turned_blocks[:, :], x_blocks[:, :]).then_inc(x_turned, 1)

            def turn_x1(i):
                if not (isinstance(i, int) and i == 0):
                    dve.wait_ge(x1_stored, 16 * i)
                cols = slice((PIECES - 1) * PIECE, O)
                dve.wait_ge(y0_summed, 3 * i + 1)
                nc.vector.transpose(x1_turned_rows[:, cols], acc0[:, PIECES - 1, 0:O - (PIECES - 1) * PIECE]
                                    ).then_inc(x1_turned, 1)
                cols = slice(0, 2 * PIECE)
                dve.wait_ge(y0_summed, 3 * i + 3)
                nc.vector.transpose(x1_turned_rows[:, cols].rearrange("p (c n) -> p c n", c=2),
                                    acc0[:, 0:2, 0:PIECE]).then_inc(x1_turned, 1)

            def g_low(j):
                dve.wait_ge(g_hi_done, j + 1)
                nc.vector.tensor_tensor(out=gT_lo[:, :], in0=g_bank[:, 0:P], in1=gT_hi[:, :].bitcast(F32),
                                        op=ALU.subtract).then_inc(g_lo_done, 1)

            turn_x(0)
            turn_weights(0)
            x_lows(0)
            weights(0, H0_AT + 1)
            dve.wait_ge(consts_made, 1)
            stack_h(0)
            weights(H0_AT + 1, OT)
            turn_x(1)
            weights(OT, OT + 1)
            x_lows(1)
            turn_x1(0)
            weights(OT + 1, H1_AT + 1)
            stack_h(1)
            weights(H1_AT + 1, X1L_AT + 1)
            x1_lows(0)
            turn_weights(X1L_AT + 1)
            weights(X1L_AT + 1, B1_LOAD)
            set_language_bias()
            b1_lows()
            with dve.Fori(1, TILES // 2) as n:
                for s in range(2):
                    i = 2 * n + s
                    turn_x(i)
                    turn_x1(i - 1)
                    gate(i - 2, n - 1)
                    g_low(i - 2)
                    stack_h(i)
                    x1_lows(i - 1)
            turn_x1(TILES - 1)
            gate(TILES - 2, BATCH - 1)
            g_low(TILES - 2)
            x1_lows(TILES - 1)
            gate(TILES - 1, BATCH - 1)
            g_low(TILES - 1)


_INS = ["x", "itok_B_0_23", "itok_B_0_7", "L0_cond_W", "L0_cond_b", "L0_cond_lora_As", "L0_cond_lora_Bs",
        "L1_cond_W", "L1_cond_Wr", "L1_cond_A", "L1_cond_B"]


def kernel(**inputs):
    import numpy as _np
    import concourse.bacc as _bacc
    from concourse import mybir as _mybir
    from concourse.bass_utils import run_bass_kernel_spmd as _run

    nc = _bacc.Bacc("TRN2", target_bir_lowering=False, num_devices=1)
    arrays, args = {}, []
    for name in _INS:
        a = _np.ascontiguousarray(inputs[name])
        arrays[f"in_{name}"] = a
        args.append(nc.dram_tensor(f"in_{name}", a.shape, _mybir.dt.from_np(a.dtype), kind="ExternalInput").ap())
    shape = inputs["x"].shape
    args.append(nc.dram_tensor("out_y", shape, _mybir.dt.float32, kind="ExternalOutput").ap())
    build(nc, *args)
    r = _run(nc, [arrays], core_ids=[0])
    return r.results[0]["out_y"]
```

```python
from contextlib import ExitStack

import concourse.bass as bass
from concourse import mybir

F32 = mybir.dt.float32
F32R = mybir.dt.float32r
I32 = mybir.dt.int32
U32 = mybir.dt.uint32
ALU = mybir.AluOpType
ACT = mybir.ActivationFunctionType

P = 128
BANK = 512
LANG_BIAS = 5.0
SCALING = 32.0 / 16.0


def build(nc, x, adapter_ids, language_ids, w0, bias0, lora_a0, lora_b0, w1, w_router, lora_a1, lora_b1, out):
    BATCH, SEQ, D = x.shape
    SLOTS, _, R0 = lora_a0.shape
    E, R1, _ = lora_a1.shape
    O = w0.shape[0]
    TILES = BATCH * SEQ // P
    KT = D // P
    OT = O // P
    PER_BANK = BANK // P
    ER = E * R1
    AR = ER + E
    PIECES = 3
    PIECE = (O + 2 * R0) // PIECES
    PIECE1 = 4 * (-(-(O + AR) // (4 * PIECES)))
    assert SEQ == 2 * P and O == D and ER == P and KT == 2 * PER_BANK and 4 * R0 == 64 and PIECES * PIECE == O + 2 * R0
    assert D == 4 * KT * 32 and PIECE % 32 == 0 and (PIECES - 1) * PIECE1 < O and PIECE1 <= BANK

    x_rows = x.rearrange("b t d -> (b t) d")
    out_rows = out.rearrange("b t d -> (b t) d")
    a1_rows = lora_a1.rearrange("e r d -> (e r) d")
    x1_scratch = nc.dram_tensor("x1_scratch", (P, D), F32, kind="Internal").ap()

    ctx = ExitStack()
    with ctx:
        def sb(name, shape, dt=F32):
            return ctx.enter_context(nc.sbuf_tensor(name, shape, dt))

        def pb(name, shape):
            return ctx.enter_context(nc.psum_tensor(name, shape, F32))

        def sem(name):
            return ctx.enter_context(nc.semaphore(name))

        w0_hi, w0_lo = sb("w0_hi", [P, KT, O + 2 * R0], F32R), sb("w0_lo", [P, KT, O], F32R)
        a0 = w0_hi[:, :, O:O + 2 * R0]
        w1_hi, w1_lo = sb("w1_hi", [P, KT, O + AR], F32R), sb("w1_lo", [P, KT, O + AR], F32R)
        b1_hi, b1_lo = sb("b1_hi", [P, O], F32R), sb("b1_lo", [P, O], F32R)
        a0_raw = sb("a0_raw", [P, KT, R0])
        b0_raw = sb("b0_raw", [P, O])
        b0 = sb("b0", [P, O], F32R)
        x_blocks, x_turned_blocks = sb("x_blocks", [P, D]), sb("x_turned_blocks", [P, D])
        xT_hi, xT_lo = sb("xT_hi", [P, KT, P], F32R), sb("xT_lo", [P, KT, P], F32R)
        x1_turned_rows, x1_turned_blocks = sb("x1_turned_rows", [P, D]), sb("x1_turned_blocks", [P, D])
        x1T_hi, x1T_lo = sb("x1T_hi", [P, KT, P], F32R), sb("x1T_lo", [P, KT, P], F32R)
        outs = sb("outs", [P, 2, O])
        stage = sb("stage", [P, 2, D])
        h_part = sb("h_part", [P, R0])
        h_nat = sb("h_nat", [P, R0])
        h_stack = sb("h_stack", [P, 4, 32])
        hT = sb("hT", [P, P], F32R)
        h1_nat = sb("h1_nat", [P, ER])
        logits = sb("logits", [P, E])
        top = sb("top", [P, 8])
        top_index = sb("top_index", [P, 8], U32)
        top_index_f = sb("top_index_f", [P, 2])
        top_gap = sb("top_gap", [P, 1])
        top_exp = sb("top_exp", [P, 1])
        exp_sum = sb("exp_sum", [P, 1])
        exp_inv = sb("exp_inv", [P, 1])
        top_gate = sb("top_gate", [P, 2])
        gate_each = sb("gate_each", [P, 2, E])
        gates = sb("gates", [P, E])
        gated = sb("gated", [P, ER])
        gT_hi, gT_lo = sb("gT_hi", [P, P], F32R), sb("gT_lo", [P, P], F32R)
        ident = sb("ident", [P, P])
        one = sb("one", [P, 1])
        experts = sb("experts", [P, E])
        languages = sb("languages", [P, BATCH], I32)
        languages_f = sb("languages_f", [P, BATCH])
        language_bias = sb("language_bias", [P, BATCH, E])
        adapters = sb("adapters", [1, BATCH], I32)

        acc0 = pb("acc0", [P, PIECES, BANK])
        h_sum = acc0[:, PIECES - 1, O - (PIECES - 1) * PIECE:PIECE]
        acc1 = pb("acc1", [P, PIECES, BANK])
        ar_sum = acc1[:, PIECES - 1, O - (PIECES - 1) * PIECE1:O - (PIECES - 1) * PIECE1 + AR]
        h_bank = pb("h_bank", [P, BANK])
        g_bank = pb("g_bank", [P, BANK])

        ids_in = sem("ids_in")
        languages_in = sem("languages_in")
        bias_in = sem("bias_in")
        x_in = sem("x_in")
        x1_stored, x1_in = sem("x1_stored"), sem("x1_in")
        a0_in, b0_in = sem("a0_in"), sem("b0_in")
        pair_in = [sem("pair_in_stage"), sem("pair_in_outs")]
        single_in = [sem(f"single_in{s}") for s in range(3)]
        out_stored = [sem("out_stored_even"), sem("out_stored_odd")]
        ident_made, consts_made, b0_cleared = sem("ident_made"), sem("consts_made"), sem("b0_cleared")
        pool_step = sem("pool_step")
        one_added, w_lo_by_pool, b1_lo_done = sem("one_added"), sem("w_lo_by_pool"), sem("b1_lo_done")
        a0_split, b0_split = sem("a0_split"), sem("b0_split")
        b1_turned = sem("b1_turned")
        x0_used, x1_used = sem("x0_used"), sem("x1_used")
        h_summed, h_turned, y0_summed = sem("h_summed"), sem("h_turned"), sem("y0_summed")
        ar_summed, g_turned, y1_summed = sem("ar_summed"), sem("g_turned"), sem("y1_summed")
        w_hi_done = sem("w_hi_done")
        b1_ordered, b1_out, b1_hi_done = sem("b1_ordered"), sem("b1_out"), sem("b1_hi_done")
        x_hi_done, x1_hi_done = sem("x_hi_done"), sem("x1_hi_done")
        h_part_done, hT_done, b0_hi_done = sem("h_part_done"), sem("hT_done"), sem("b0_hi_done")
        exp_done, g_hi_done, out_done = sem("exp_done"), sem("g_hi_done"), sem("out_done")
        w_turned, x_turned, x1_turned = sem("w_turned"), sem("x_turned"), sem("x1_turned")
        w_lo_by_dve = sem("w_lo_by_dve")
        x_lo_done, x1_lo_done = sem("x_lo_done"), sem("x1_lo_done")
        h_stacked, gap_done, gated_done, g_lo_done = sem("h_stacked"), sem("gap_done"), sem("gated_done"), sem("g_lo_done")
        setup_step, h_step, gate_step = sem("setup_step"), sem("h_step"), sem("gate_step")

        loads = ([("w0", t) for t in (6, 7, 5, 4, 3, 2, 1, 0)] + [("a1", 0)] + [("w1", t) for t in range(OT - 2, OT)]
                 + [("router", 0)] + [("w1", t) for t in range(OT - 2)])
        B1_LOAD = len(loads)
        def parts_of_x(i):
            return (x1T_hi, x1T_lo) if isinstance(i, int) and i == 0 else (xT_hi, xT_lo)

        def parts_of_x1(i):
            return (xT_hi, xT_lo) if isinstance(i, int) and i == TILES - 1 else (x1T_hi, x1T_lo)

        singles = [stage[:, 0, :], stage[:, 1, :], x_blocks[:, :]]
        x1_buffers = [x1_turned_rows[:, :], x1_turned_blocks[:, :]]

        B1_PLACE = B1_LOAD - 2

        def place(u):
            return B1_PLACE if u == B1_LOAD else u if u < B1_PLACE else u + 1

        def single_slot(u):
            return u if u < 2 else (place(u) - OT) % 3

        def raw_slot(u):
            if 2 <= u < OT:
                return (stage, outs)[u // 2 % 2][:, 1 - u % 2, :]
            return singles[single_slot(u)]

        def turned_slot(u):
            return x1_buffers[u % 2] if u < OT else outs[:, u % 2, :]

        def wait_raw_free(engine, u):
            if u < OT:
                if u >= 4:
                    engine.wait_ge(w_turned, u - 2)
            elif u == OT + 2:
                engine.wait_ge(x_turned, 2)
            else:
                engine.wait_ge(w_turned, OT - 2 if u < OT + 2 else place(u) - 2)

        def wait_raw(engine, u):
            if u < 2:
                engine.wait_ge(single_in[single_slot(u)], 64)
            elif u < OT:
                engine.wait_ge(pair_in[u // 2 % 2], 64 * (u // 4 + (u // 2 % 2)))
            else:
                before = (place(u) - OT) // 3 + (1 if single_slot(u) < 2 else 0)
                engine.wait_ge(single_in[single_slot(u)], 64 * before + (16 if u == B1_LOAD else 64))

        def wait_turned_free(engine, u):
            if OT <= u < OT + 2:
                engine.wait_ge(w_turned, OT)
            elif u >= 2:
                wait_split(engine, u - 1)

        def gets_one(u):
            return loads[u][0] in ("w0", "w1")

        def additions(u):
            return len([v for v in range(u + 1) if gets_one(v)])

        def loaded_through(names):
            return 1 + max(u for u, load in enumerate(loads) if load in names)

        pool_lows = (4, 6, 9, 14, 16)

        def wait_split(engine, count):
            by_pool = len([u for u in range(count) if u in pool_lows])
            if count > by_pool:
                engine.wait_ge(w_lo_by_dve, count - by_pool)
            if by_pool:
                engine.wait_ge(w_lo_by_pool, by_pool)

        H0_AT, H1_AT, X1L_AT = OT - 3, OT + 4, OT + 6
        LATE = (3, OT - 2, OT, OT + 7)
        assert H0_AT < OT <= H1_AT < X1L_AT < B1_LOAD

        b1_staged, b1_rows = raw_slot(B1_LOAD), b0_raw[:, :]

        def in_place(blocks, ks=slice(0, KT)):
            return blocks.rearrange("p (b k j) -> p b k j", b=4, k=KT)[:, :, ks, :]

        def chunks(target, ks=slice(0, KT)):
            return target[:, ks, :].rearrange("p k (b j) -> p b k j", b=4)

        def weight_target(u, w):
            kind, t = loads[u]
            turned = turned_slot(u)
            if kind == "router":
                return w[1][:, :, O + ER:O + AR], turned[:, 0:KT * 32].rearrange("p (k j) -> p k j", k=KT)[:, :, 0:E]
            start = {"w0": t * P, "w1": t * P, "a1": O}[kind]
            return chunks(w[kind != "w0"][:, :, start:start + P]), in_place(turned)

        def b1_target(b1):
            return b1[:, :].rearrange("q (p j) -> q j p", j=OT)

        def b1_bank(g):
            return (h_bank, g_bank)[g][:, :].rearrange("p (k n) -> p k n", k=PER_BANK)

        def b1_blocks(g=None):
            blocks = b0_raw[:, :].rearrange("q (j p) -> q j p", j=OT)
            return blocks if g is None else blocks[:, g * PER_BANK:(g + 1) * PER_BANK, :]

        LAST_PIECES = [(piece, slice(piece * PIECE1, min((piece + 1) * PIECE1, O))) for piece in (PIECES - 1, 0, 1)]

        block = ctx.enter_context(nc.Block())

        @block.sync
        def _(sp):
            def load_blocks(dst, src, arrived):
                for a in range(4):
                    sp.dma_start(dst[32 * a:32 * a + 32, :].rearrange("j (b n) -> j b n", b=4),
                                 src[:, D // 4 * a:D // 4 * (a + 1)].rearrange("(b j) n -> j b n", b=4)
                                 ).then_inc(arrived, 16)

            def load_weights(u):
                wait_raw_free(sp, u)
                slot = raw_slot(u)
                arrived = single_in[single_slot(u)]
                if u == B1_LOAD:
                    sp.dma_start(slot.rearrange("p (e n) -> p e n", e=E),
                                 lora_b1.rearrange("e (p j) r -> p e (j r)", p=P)).then_inc(arrived, 16)
                    return
                kind, t = loads[u]
                if kind == "router":
                    for a in range(4):
                        sp.dma_start(slot[32 * a:32 * a + E, 0:D // 4], w_router[:, D // 4 * a:D // 4 * (a + 1)]
                                     ).then_inc(arrived, 16)
                else:
                    rows = {"w0": w0, "w1": w1, "a1": a1_rows}[kind]
                    load_blocks(slot, rows[t * P:(t + 1) * P, :], arrived)

            def load_pair(u):
                wait_raw_free(sp, u)
                t = loads[u + 1][1]
                pair = (stage, outs)[u // 2 % 2]
                for a in range(4):
                    sp.dma_start(pair[32 * a:32 * a + 32, :, :].rearrange("j s (b n) -> j (s b) n", b=4),
                                 w0[t * P:(t + 2) * P, D // 4 * a:D // 4 * (a + 1)].rearrange(
                                     "(b j) n -> j b n", b=8)).then_inc(pair_in[u // 2 % 2], 16)

            def load_x(i):
                load_blocks(x_blocks[:, :], x_rows[bass.ds(i * P, P), :], x_in)

            def store_x1(i):
                sp.wait_ge(x1_turned, 2 * i + 2)
                sp.dma_start(x1_scratch, x1_turned_rows[:, :]).then_inc(x1_stored, 16)

            def place_x1(i):
                sp.wait_ge(x1_stored, 16 * (i + 1))
                load_blocks(x1_turned_blocks[:, :], x1_scratch, x1_in)

            def slot_id(b):
                return sp.value_load(adapters[0:1, bass.ds(b, 1)], min_val=0, max_val=SLOTS - 1)

            def load_a0(s):
                for a in range(4):
                    sp.dma_start(a0_raw[32 * a:32 * a + 32, :, :],
                                 lora_a0[bass.ds(s, 1), D // 4 * a:D // 4 * (a + 1), :].rearrange(
                                     "s (k c) r -> c (s k) r", k=KT)).then_inc(a0_in, 16)

            def load_b0(s):
                for row in (0, R0, 64, 64 + R0):
                    sp.dma_start(b0_raw[row:row + R0, :],
                                 lora_b0[bass.ds(s, 1), :, :].rearrange("s r o -> (s r) o")).then_inc(b0_in, 16)

            def store_out(i, slot):
                sp.wait_ge(out_done, 2 * (i + 1))
                sp.dma_start(out_rows[bass.ds(i * P, P), :], outs[:, slot, :]).then_inc(out_stored[slot], 16)

            sp.dma_start(adapters[0:1, :], adapter_ids.rearrange("(a b) -> a b", a=1)).then_inc(ids_in, 16)
            load_x(0)
            for u in range(2):
                load_weights(u)
            sp.wait_ge(ids_in, 16)
            first_id = slot_id(0)
            load_pair(2)
            load_a0(first_id)
            load_pair(4)
            load_pair(6)
            sp.wait_ge(b0_cleared, 1)
            load_b0(first_id)
            for row in (32, 96):
                sp.dma_start(b0_raw[row:row + 1, :], bias0.rearrange("(a b) -> a b", a=1)).then_inc(bias_in, 16)
            sp.dma_start(languages[:, :], language_ids.rearrange("(a b) -> a b", a=1).to_broadcast([P, BATCH])
                         ).then_inc(languages_in, 16)
            sp.wait_ge(x_turned, 1)
            load_x(1)
            for u in range(OT, OT + 5):
                load_weights(u)
            store_x1(0)
            for u in range(OT + 5, OT + 7):
                load_weights(u)
            wait_split(sp, OT)
            place_x1(0)
            for u in range(OT + 7, B1_PLACE):
                load_weights(u)
            load_weights(B1_LOAD)
            for u in range(B1_PLACE, B1_LOAD):
                load_weights(u)
            sp.wait_ge(b1_ordered, 1)
            for slot in range(2):
                sp.sem_inc(out_stored[slot], 16)
            with sp.Fori(1, TILES // 2) as n:
                s = slot_id(n)
                for slot in range(2):
                    i = 2 * n + slot
                    sp.wait_ge(x_turned, i)
                    load_x(i)
                    if slot == 0:
                        sp.wait_ge(a0_split, n)
                        load_a0(s)
                        sp.wait_ge(b1_lo_done, 1)
                        sp.wait_ge(b0_split, n)
                        load_b0(s)
                    store_x1(i - 1)
                    place_x1(i - 1)
                    store_out(i - 2, slot)
            store_x1(TILES - 1)
            place_x1(TILES - 1)
            store_out(TILES - 2, 0)
            for k, (_, cols) in enumerate(LAST_PIECES):
                sp.wait_ge(out_done, 2 * (TILES - 1) + k + 1)
                sp.dma_start(out_rows[(TILES - 1) * P:TILES * P, cols], outs[:, 1, cols]).then_inc(out_stored[1], 16)
            sp.wait_ge(out_stored[0], 16 * (TILES // 2 + 1))
            sp.wait_ge(out_stored[1], 16 * (TILES // 2 + len(LAST_PIECES)))

        @block.gpsimd
        def _(pool):
            steps = [0]

            def link(ins):
                steps[0] += 1
                ins.then_inc(pool_step, 1)
                pool.wait_ge(pool_step, steps[0])

            link(nc.gpsimd.memset(ident[:, :], 0.0))
            nc.gpsimd.affine_select(out=ident[:, :], in_=ident[:, :], compare_op=ALU.not_equal, fill=1.0, base=0,
                                    pattern=[[-1, P]], channel_multiplier=1).then_inc(ident_made, 1)
            pool.wait_ge(ident_made, 1)
            nc.gpsimd.memset(b0_raw[:, :], 0.0).then_inc(b0_cleared, 1)
            pool.wait_ge(b0_cleared, 1)
            link(nc.gpsimd.memset(one[:, :], 1.0))
            link(nc.gpsimd.memset(h_stack[:, :, :], 0.0))
            link(nc.gpsimd.memset(h_stack[:, 1:4:2, 0:1], 1.0))
            nc.gpsimd.iota(experts[:, :], pattern=[[1, E]], base=0, channel_multiplier=0,
                           allow_small_or_imprecise_dtypes=True).then_inc(consts_made, 1)
            pool.wait_ge(consts_made, 1)

            def split_a0(b, done):
                pool.wait_ge(a0_in, 64 * (b + 1))
                nc.gpsimd.tensor_tensor(out=a0[:, :, 0:R0], in0=a0_raw[:, :, :],
                                        in1=one[:, :].rearrange("p (a b) -> p a b", a=1).to_broadcast([P, KT, R0]),
                                        op=ALU.mult).then_inc(pool_step, 1)
                pool.wait_ge(pool_step, done)
                nc.gpsimd.tensor_tensor(out=a0[:, :, R0:2 * R0], in0=a0_raw[:, :, :],
                                        in1=a0[:, :, 0:R0].bitcast(F32), op=ALU.subtract).then_inc(a0_split, 1)
                pool.wait_ge(a0_split, b + 1)

            def split_b0(b, done):
                pool.wait_ge(b0_in, 64 * (b + 1))
                for k, first in enumerate((0, 64)):
                    nc.gpsimd.tensor_tensor(out=b0[first:first + 32, :], in0=b0_raw[first:first + 32, :],
                                            in1=one[first:first + 32, :].to_broadcast([32, O]),
                                            op=ALU.mult).then_inc(pool_step, 1)
                    pool.wait_ge(pool_step, done + k)
                nc.gpsimd.tensor_tensor(out=b0[64:96, :], in0=b0_raw[64:96, :],
                                        in1=b0[64:96, :].bitcast(F32), op=ALU.subtract).then_inc(b0_split, 1)
                pool.wait_ge(b0_split, b + 1)

            def x_low(i):
                for bank in range(2):
                    ks = slice(bank * PER_BANK, (bank + 1) * PER_BANK)
                    pool.wait_ge(x_hi_done, 2 * i + bank + 1)
                    nc.gpsimd.tensor_tensor(out=chunks(xT_lo, ks), in0=in_place(x_turned_blocks[:, :], ks),
                                            in1=chunks(xT_hi, ks).bitcast(F32), op=ALU.subtract).then_inc(x_lo_done, 1)
                    pool.wait_ge(x_lo_done, 2 * i + bank + 1)

            def add_one(u):
                t = loads[u][1]
                wait_raw(pool, u)
                group = slice(32 * (t // 2), 32 * (t // 2) + 32)
                first = raw_slot(u)[group, 128 * (t % 2):128 * (t % 2) + 32]
                diagonal = bass.AP(tensor=first.tensor, offset=first.offset,
                                   ap=[list(first.ap[0]), [D // 4 + 32, 4], [1, 32]])
                ones = ident[group, group].rearrange("p (a n) -> p a n", a=1).to_broadcast([32, 4, 32])
                nc.gpsimd.tensor_tensor(out=diagonal, in0=diagonal, in1=ones, op=ALU.add).then_inc(one_added, 1)
                pool.wait_ge(one_added, additions(u))

            def low_weights(u):
                pool.wait_ge(w_hi_done, u + 1)
                lo, src = weight_target(u, (w0_lo, w1_lo))
                hi, _ = weight_target(u, (w0_hi, w1_hi))
                nc.gpsimd.tensor_tensor(out=lo, in0=src, in1=hi.bitcast(F32), op=ALU.subtract).then_inc(w_lo_by_pool, 1)
                pool.wait_ge(w_lo_by_pool, len([v for v in pool_lows if v <= u]))

            add_one(0)
            add_one(1)
            add_one(2)
            add_one(3)
            split_a0(0, steps[0] + 1)
            add_one(4)
            add_one(5)
            low_weights(4)
            add_one(6)
            add_one(7)
            low_weights(6)
            pool.wait_ge(b0_hi_done, 1)
            add_one(OT + 1)
            nc.gpsimd.tensor_tensor(out=b0[64:128, :], in0=b0_raw[64:128, :],
                                    in1=b0[64:128, :].bitcast(F32), op=ALU.subtract).then_inc(b0_split, 1)
            pool.wait_ge(b0_split, 1)
            for u in range(OT + 2, B1_LOAD):
                if gets_one(u):
                    add_one(u)
                if u - 1 in pool_lows:
                    low_weights(u - 1)
            pool.wait_ge(b1_hi_done, 1)
            nc.gpsimd.tensor_tensor(out=b1_target(b1_lo), in0=b1_blocks(), in1=b1_target(b1_hi).bitcast(F32),
                                    op=ALU.subtract).then_inc(b1_lo_done, 1)
            pool.wait_ge(b1_lo_done, 1)
            base = steps[0] + 2
            with pool.Fori(1, TILES // 2) as n:
                pool.wait_ge(h_summed, 2 * n)
                split_a0(n, 3 * n + (base - 3))
                x_low(2 * n)
                pool.wait_ge(y0_summed, PIECES * 2 * n)
                split_b0(n, 3 * n + (base - 2))
                x_low(2 * n + 1)

        @block.tensor
        def _(pe):
            def turn_b1():
                pe.wait_ge(b1_ordered, 1)
                for g in range(2):
                    for k in range(PER_BANK):
                        j = g * PER_BANK + k
                        last = nc.tensor.transpose(b1_bank(g)[:, k, :], b1_rows[:, j * P:(j + 1) * P], ident[:, :])
                    last.then_inc(b1_turned, 1)

            def base0(i, piece, end_of_tile=1):
                start = piece * PIECE
                low_end = min(start + PIECE, O)
                last_piece = piece == PIECES - 1
                bank = acc0[:, piece, :]
                x_hi, x_lo = parts_of_x(i)
                for k in range(KT):
                    nc.tensor.matmul(bank[:, 0:PIECE], x_hi[:, k, :], w0_hi[:, k, start:start + PIECE],
                                     start=(k == 0), stop=False)
                    nc.tensor.matmul(bank[:, 0:low_end - start], x_hi[:, k, :], w0_lo[:, k, start:low_end],
                                     start=False, stop=False)
                    last = nc.tensor.matmul(bank[:, 0:PIECE], x_lo[:, k, :], w0_hi[:, k, start:start + PIECE],
                                            start=False, stop=last_piece and k == KT - 1)
                if last_piece:
                    last.then_inc(h_summed, 1)
                if piece == end_of_tile:
                    last.then_inc(x0_used, 1)

            def tile_ready(i, b):
                pe.wait_ge(x_lo_done, 2 * i + 2)
                pe.wait_ge(x1_turned, 2 * i - 1)
                pe.wait_ge(a0_split, b + 1)

            def base1(j, piece):
                last_piece = piece == PIECES - 1
                if last_piece:
                    pe.wait_ge(x1_lo_done, 2 * j + 2)
                    if not (isinstance(j, int) and j == 0):
                        pe.wait_ge(out_done, 2 * j)
                x1_hi, x1_lo = parts_of_x1(j)
                start, end = piece * PIECE1, min((piece + 1) * PIECE1, O + AR)
                for k in range(KT):
                    for x_part, w_part in ((x1_hi, w1_hi), (x1_hi, w1_lo), (x1_lo, w1_hi)):
                        final = k == KT - 1 and x_part is x1_lo
                        last = nc.tensor.matmul(acc1[:, piece, 0:end - start], x_part[:, k, :],
                                                w_part[:, k, start:end], start=(k == 0 and w_part is w1_hi and x_part is x1_hi),
                                                stop=last_piece and final)
                if last_piece:
                    last.then_inc(ar_summed, 1)
                if piece == 1:
                    last.then_inc(x1_used, 1)

            def turn_h(i):
                pe.wait_ge(h_stacked, i + 1)
                nc.tensor.transpose(h_bank[:, 0:P], h_stack[:, :, :].rearrange("p a b -> p (a b)"),
                                    ident[:, :]).then_inc(h_turned, 1)

            def lora0(i, b):
                pe.wait_ge(hT_done, i + 1)
                pe.wait_ge(b0_split, b + 1)
                for piece in (PIECES - 1, 0, 1):
                    start, end = piece * PIECE, min((piece + 1) * PIECE, O)
                    nc.tensor.matmul(acc0[:, piece, 0:end - start], hT[:, :], b0[:, start:end], start=False,
                                     stop=True, skip_group_check=(piece == PIECES - 1)).then_inc(y0_summed, 1)

            def turn_g(j):
                pe.wait_ge(gated_done, j + 1)
                nc.tensor.transpose(g_bank[:, 0:P], gated[:, :], ident[:, :]).then_inc(g_turned, 1)

            def lora1(j):
                pe.wait_ge(b1_lo_done, 1)
                pe.wait_ge(g_lo_done, j + 1)
                for piece in (PIECES - 1, 0, 1):
                    start, end = piece * PIECE1, min((piece + 1) * PIECE1, O)
                    for g_part, b_part in ((gT_hi, b1_hi), (gT_hi, b1_lo), (gT_lo, b1_hi)):
                        final = g_part is gT_lo
                        last = nc.tensor.matmul(acc1[:, piece, 0:end - start], g_part[:, :], b_part[:, start:end],
                                                start=False, stop=final, skip_group_check=(piece == PIECES - 1))
                    last.then_inc(y1_summed, 1)

            pe.wait_ge(ident_made, 1)
            pe.wait_ge(x_lo_done, 2)
            pe.wait_ge(a0_split, 1)
            for piece in (2, 1, 0):
                tiles = range(piece * PIECE // P, min((piece + 1) * PIECE - 1, O - 1) // P + 1)
                wait_split(pe, loaded_through([("w0", t) for t in tiles]))
                base0(0, piece, end_of_tile=0)
                if piece == 1:
                    turn_h(0)
            lora0(0, 0)
            tile_ready(1, 0)
            base0(1, 2)
            pe.wait_ge(x1_turned, 2)
            base0(1, 0)
            turn_h(1)
            base0(1, 1)
            lora0(1, 0)
            for piece in (2, 0, 1):
                tiles = range(piece * PIECE1 // P, min((piece + 1) * PIECE1 - 1, O - 1) // P + 1)
                wait_split(pe, loaded_through([("w1", t) for t in tiles] + [("a1", 0), ("router", 0)]))
                base1(0, piece)
                if piece == 2:
                    turn_b1()
            pe.wait_ge(b1_out, 2)
            turn_g(0)
            with pe.Fori(1, TILES // 2) as n:
                for s in range(2):
                    i = 2 * n + s
                    tile_ready(i, n)
                    base0(i, 2)
                    lora1(i - 2)
                    pe.wait_ge(x1_turned, 2 * i)
                    base0(i, 0)
                    turn_h(i)
                    base0(i, 1)
                    lora0(i, n)
                    base1(i - 1, 2)
                    base1(i - 1, 0)
                    base1(i - 1, 1)
                    turn_g(i - 1)
            lora1(TILES - 2)
            base1(TILES - 1, 2)
            base1(TILES - 1, 0)
            base1(TILES - 1, 1)
            turn_g(TILES - 1)
            lora1(TILES - 1)

        @block.scalar
        def _(act):
            def copy(dst, src, scale=1.0):
                return nc.scalar.activation(dst, src, ACT.Copy, scale=scale)

            def high_weights(lo, hi):
                for u in range(lo, hi):
                    act.wait_ge(w_turned, u + 1)
                    dst, src = weight_target(u, (w0_hi, w1_hi))
                    copy(dst, src).then_inc(w_hi_done, 1)

            def split_b1():
                act.wait_ge(b1_turned, 2)
                for g in range(2):
                    copy(b1_blocks(g), b1_bank(g)).then_inc(b1_out, 1)
                act.wait_ge(b1_out, 2)
                copy(b1_target(b1_hi), b1_blocks()).then_inc(b1_hi_done, 1)

            def x_highs(i):
                act.wait_ge(x_turned, i + 1)
                if not isinstance(i, int):
                    act.wait_ge(x0_used, i)
                for bank in range(2):
                    ks = slice(bank * PER_BANK, (bank + 1) * PER_BANK)
                    copy(chunks(parts_of_x(i)[0], ks), in_place(x_turned_blocks[:, :], ks)).then_inc(x_hi_done, 1)

            def x1_highs(i):
                act.wait_ge(x1_in, 64 * (i + 1))
                if isinstance(i, int) and i == 0:
                    act.wait_ge(x0_used, 1)
                elif isinstance(i, int) and i == TILES - 1:
                    act.wait_ge(x0_used, TILES)
                else:
                    act.wait_ge(x1_used, i)
                for bank in range(2):
                    ks = slice(bank * PER_BANK, (bank + 1) * PER_BANK)
                    copy(chunks(parts_of_x1(i)[0], ks), in_place(x1_turned_blocks[:, :], ks)).then_inc(x1_hi_done, 1)

            def y_out(j, slot, stores_before):
                act.wait_ge(out_stored[slot], 16 * (stores_before + 1))
                cols = slice((PIECES - 1) * PIECE1, O)
                act.wait_ge(y1_summed, 3 * j + 1)
                copy(outs[:, slot, cols], acc1[:, PIECES - 1, 0:O - (PIECES - 1) * PIECE1]).then_inc(out_done, 1)
                cols = slice(0, 2 * PIECE1)
                act.wait_ge(y1_summed, 3 * j + 3)
                copy(outs[:, slot, cols].rearrange("p (c n) -> p c n", c=2), acc1[:, 0:2, 0:PIECE1]
                     ).then_inc(out_done, 1)

            def last_out():
                act.wait_ge(out_stored[1], 16 * (TILES // 2))
                for k, (piece, cols) in enumerate(LAST_PIECES):
                    act.wait_ge(y1_summed, 3 * (TILES - 1) + k + 1)
                    copy(outs[:, 1, cols], acc1[:, piece, 0:cols.stop - cols.start]).then_inc(out_done, 1)

            def h_low_part(i):
                act.wait_ge(h_summed, i + 1)
                copy(h_part[:, :], h_sum[:, R0:2 * R0], scale=SCALING).then_inc(h_part_done, 1)

            def exp_gap(j):
                act.wait_ge(gap_done, j + 1)
                nc.scalar.activation(top_exp[:, :], top_gap[:, :], ACT.Exp).then_inc(exp_done, 1)

            def h_out(i):
                act.wait_ge(h_turned, i + 1)
                copy(hT[:, :], h_bank[:, 0:P]).then_inc(hT_done, 1)

            def g_high(j):
                act.wait_ge(g_turned, j + 1)
                copy(gT_hi[:, :], g_bank[:, 0:P]).then_inc(g_hi_done, 1)

            x_highs(0)
            high_weights(0, H0_AT + 1)
            h_low_part(0)
            high_weights(H0_AT + 1, OT)
            act.wait_ge(b0_in, 64)
            act.wait_ge(bias_in, 32)
            copy(b0[:, :], b0_raw[:, :]).then_inc(b0_hi_done, 1)
            h_out(0)
            x_highs(1)
            high_weights(OT, H1_AT + 1)
            h_low_part(1)
            high_weights(H1_AT + 1, X1L_AT)
            h_out(1)
            x1_highs(0)
            high_weights(X1L_AT, X1L_AT + 1)
            high_weights(X1L_AT + 1, B1_PLACE)
            wait_raw(act, B1_LOAD)
            act.wait_ge(b0_split, 1)
            copy(b1_rows.rearrange("p (j e r) -> p e j r", j=OT, e=E),
                 b1_staged.rearrange("p (e j r) -> p e j r", e=E, j=OT)).then_inc(b1_ordered, 1)
            high_weights(B1_PLACE, B1_LOAD - 1)
            split_b1()
            high_weights(B1_LOAD - 1, B1_LOAD)
            with act.Fori(1, TILES // 2) as n:
                for s in range(2):
                    i = 2 * n + s
                    x_highs(i)
                    exp_gap(i - 2)
                    g_high(i - 2)
                    h_low_part(i)
                    x1_highs(i - 1)
                    y_out(i - 2, s, n - 1)
                    h_out(i)
            exp_gap(TILES - 2)
            x1_highs(TILES - 1)
            g_high(TILES - 2)
            y_out(TILES - 2, 0, TILES // 2 - 1)
            exp_gap(TILES - 1)
            g_high(TILES - 1)
            last_out()

        @block.vector
        def _(dve):
            def turn_weights(u):
                if gets_one(u):
                    dve.wait_ge(one_added, additions(u))
                else:
                    wait_raw(dve, u)
                wait_turned_free(dve, u)
                size = KT * 32 if loads[u][0] == "router" else D
                nc.vector.transpose(turned_slot(u)[:, 0:size], raw_slot(u)[:, 0:size]
                                    ).then_inc(w_turned, 1)

            def low_weights(u):
                if u in pool_lows:
                    return
                dve.wait_ge(w_hi_done, u + 1)
                lo, src = weight_target(u, (w0_lo, w1_lo))
                hi, _ = weight_target(u, (w0_hi, w1_hi))
                nc.vector.tensor_tensor(out=lo, in0=src, in1=hi.bitcast(F32), op=ALU.subtract).then_inc(w_lo_by_dve, 1)

            def weights(lo, hi):
                for u in range(lo, hi):
                    if u + 1 < B1_LOAD and u + 1 not in LATE:
                        turn_weights(u + 1)
                    low_weights(u)

            def x_lows(i):
                for bank in range(2):
                    ks = slice(bank * PER_BANK, (bank + 1) * PER_BANK)
                    dve.wait_ge(x_hi_done, 2 * i + bank + 1)
                    nc.vector.tensor_tensor(out=chunks(parts_of_x(i)[1], ks), in0=in_place(x_turned_blocks[:, :], ks),
                                            in1=chunks(parts_of_x(i)[0], ks).bitcast(F32), op=ALU.subtract).then_inc(x_lo_done, 1)

            def x1_lows(i):
                for bank in range(2):
                    ks = slice(bank * PER_BANK, (bank + 1) * PER_BANK)
                    dve.wait_ge(x1_hi_done, 2 * i + bank + 1)
                    nc.vector.tensor_tensor(out=chunks(parts_of_x1(i)[1], ks), in0=in_place(x1_turned_blocks[:, :], ks),
                                            in1=chunks(parts_of_x1(i)[0], ks).bitcast(F32), op=ALU.subtract
                                            ).then_inc(x1_lo_done, 1)

            def stack_h(i):
                dve.wait_ge(h_part_done, i + 1)
                nc.vector.scalar_tensor_tensor(out=h_nat[:, :], in0=h_sum[:, 0:R0], scalar=SCALING,
                                               in1=h_part[:, :], op0=ALU.mult, op1=ALU.add).then_inc(h_step, 1)
                twice = h_nat[:, :].rearrange("p (a r) -> p a r", a=1).to_broadcast([P, 2, R0])
                dve.wait_ge(h_step, 2 * i + 1)
                nc.vector.tensor_copy(h_stack[:, 0:3:2, 0:R0].bitcast(F32R), twice).then_inc(h_step, 1)
                dve.wait_ge(h_step, 2 * i + 2)
                nc.vector.tensor_tensor(out=h_stack[:, 0:3:2, R0:2 * R0], in0=twice, in1=h_stack[:, 0:3:2, 0:R0],
                                        op=ALU.subtract).then_inc(h_stacked, 1)

            def set_language_bias():
                dve.wait_ge(languages_in, 16)
                dve.wait_ge(consts_made, 1)
                nc.vector.tensor_copy(languages_f[:, :], languages[:, :]).then_inc(setup_step, 1)
                dve.wait_ge(setup_step, 1)
                nc.vector.tensor_tensor(
                    out=language_bias[:, :, :],
                    in0=experts[:, :].rearrange("p (a e) -> p a e", a=1).to_broadcast([P, BATCH, E]),
                    in1=languages_f[:, :].rearrange("p (b a) -> p b a", a=1).to_broadcast([P, BATCH, E]),
                    op=ALU.is_equal).then_inc(setup_step, 1)
                dve.wait_ge(setup_step, 2)
                nc.vector.tensor_scalar(language_bias[:, :, :], language_bias[:, :, :], LANG_BIAS, None,
                                        ALU.mult).then_inc(setup_step, 1)
                dve.wait_ge(setup_step, 3)

            GATE_STEPS = 12

            def gate(j, b):
                step = [0]

                def mark(ins):
                    step[0] += 1
                    ins.then_inc(gate_step, 1)

                def link(ins):
                    mark(ins)
                    dve.wait_ge(gate_step, GATE_STEPS * j + step[0])

                dve.wait_ge(ar_summed, j + 1)
                link(nc.vector.tensor_tensor(out=logits[:, :], in0=ar_sum[:, ER:AR],
                                             in1=language_bias[:, bass.ds(b, 1), :].rearrange("p a e -> p (a e)"),
                                             op=ALU.add))
                mark(nc.vector.tensor_copy(h1_nat[:, :], ar_sum[:, 0:ER]))
                link(nc.vector.max(out=top[:, :], in_=logits[:, :]))
                nc.vector.tensor_tensor(out=top_gap[:, :], in0=top[:, 1:2], in1=top[:, 0:1],
                                        op=ALU.subtract).then_inc(gap_done, 1)
                link(nc.vector.max_index(out=top_index[:, :], in_max=top[:, :], in_values=logits[:, :]))
                mark(nc.vector.tensor_copy(top_index_f[:, :], top_index[:, 0:2]))
                dve.wait_ge(exp_done, j + 1)
                link(nc.vector.tensor_scalar(exp_sum[:, :], top_exp[:, :], 1.0, None, ALU.add))
                link(nc.vector.reciprocal(exp_inv[:, :], exp_sum[:, :]))
                mark(nc.vector.tensor_scalar(top_gate[:, 0:1], exp_inv[:, :], SCALING, None, ALU.mult))
                link(nc.vector.scalar_tensor_tensor(out=top_gate[:, 1:2], in0=top_exp[:, :], scalar=SCALING,
                                                    in1=exp_inv[:, :], op0=ALU.mult, op1=ALU.mult))
                mark(nc.vector.tensor_scalar(gate_each[:, 0, :], experts[:, :], top_index_f[:, 0:1],
                                             top_gate[:, 0:1], ALU.is_equal, ALU.mult))
                link(nc.vector.tensor_scalar(gate_each[:, 1, :], experts[:, :], top_index_f[:, 1:2],
                                             top_gate[:, 1:2], ALU.is_equal, ALU.mult))
                link(nc.vector.tensor_tensor(out=gates[:, :], in0=gate_each[:, 0, :], in1=gate_each[:, 1, :],
                                             op=ALU.add))
                assert step[0] == GATE_STEPS
                nc.vector.tensor_tensor(
                    out=gated[:, :].rearrange("p (e r) -> p e r", e=E),
                    in0=h1_nat[:, :].rearrange("p (e r) -> p e r", e=E),
                    in1=gates[:, :].rearrange("p (e a) -> p e a", a=1).to_broadcast([P, E, R1]),
                    op=ALU.mult).then_inc(gated_done, 1)

            def turn_x(i):
                dve.wait_ge(x_in, 64 * (i + 1))
                if not (isinstance(i, int) and i == 0):
                    dve.wait_ge(x_lo_done, 2 * i)
                nc.vector.transpose(x_turned_blocks[:, :], x_blocks[:, :]).then_inc(x_turned, 1)

            def turn_x1(i):
                if not (isinstance(i, int) and i == 0):
                    dve.wait_ge(x1_stored, 16 * i)
                cols = slice((PIECES - 1) * PIECE, O)
                dve.wait_ge(y0_summed, 3 * i + 1)
                nc.vector.transpose(x1_turned_rows[:, cols], acc0[:, PIECES - 1, 0:O - (PIECES - 1) * PIECE]
                                    ).then_inc(x1_turned, 1)
                cols = slice(0, 2 * PIECE)
                dve.wait_ge(y0_summed, 3 * i + 3)
                nc.vector.transpose(x1_turned_rows[:, cols].rearrange("p (c n) -> p c n", c=2),
                                    acc0[:, 0:2, 0:PIECE]).then_inc(x1_turned, 1)

            def g_low(j):
                dve.wait_ge(g_hi_done, j + 1)
                nc.vector.tensor_tensor(out=gT_lo[:, :], in0=g_bank[:, 0:P], in1=gT_hi[:, :].bitcast(F32),
                                        op=ALU.subtract).then_inc(g_lo_done, 1)

            turn_x(0)
            turn_weights(0)
            x_lows(0)
            weights(0, 3)
            turn_weights(3)
            weights(3, H0_AT + 1)
            dve.wait_ge(consts_made, 1)
            stack_h(0)
            turn_weights(OT - 2)
            weights(H0_AT + 1, OT - 1)
            turn_x(1)
            weights(OT - 1, OT)
            turn_weights(OT)
            x_lows(1)
            weights(OT, OT + 1)
            turn_x1(0)
            weights(OT + 1, H1_AT + 1)
            stack_h(1)
            weights(H1_AT + 1, X1L_AT + 1)
            x1_lows(0)
            set_language_bias()
            turn_weights(X1L_AT + 1)
            weights(X1L_AT + 1, B1_LOAD)
            with dve.Fori(1, TILES // 2) as n:
                for s in range(2):
                    i = 2 * n + s
                    turn_x(i)
                    turn_x1(i - 1)
                    gate(i - 2, n - 1)
                    g_low(i - 2)
                    stack_h(i)
                    x1_lows(i - 1)
            turn_x1(TILES - 1)
            gate(TILES - 2, BATCH - 1)
            x1_lows(TILES - 1)
            g_low(TILES - 2)
            gate(TILES - 1, BATCH - 1)
            g_low(TILES - 1)


_INS = ["x", "itok_B_0_23", "itok_B_0_7", "L0_cond_W", "L0_cond_b", "L0_cond_lora_As", "L0_cond_lora_Bs",
        "L1_cond_W", "L1_cond_Wr", "L1_cond_A", "L1_cond_B"]


def kernel(**inputs):
    import numpy as _np
    import concourse.bacc as _bacc
    from concourse import mybir as _mybir
    from concourse.bass_utils import run_bass_kernel_spmd as _run

    nc = _bacc.Bacc("TRN2", target_bir_lowering=False, num_devices=1)
    arrays, args = {}, []
    for name in _INS:
        a = _np.ascontiguousarray(inputs[name])
        arrays[f"in_{name}"] = a
        args.append(nc.dram_tensor(f"in_{name}", a.shape, _mybir.dt.from_np(a.dtype), kind="ExternalInput").ap())
    shape = inputs["x"].shape
    args.append(nc.dram_tensor("out_y", shape, _mybir.dt.float32, kind="ExternalOutput").ap())
    build(nc, *args)
    r = _run(nc, [arrays], core_ids=[0])
    return r.results[0]["out_y"]
```
